# Optimizing a Trainium2 kernel written in Bass

```python
import numpy as np
import jax
import jax.numpy as jnp

def _softmax(x, axis=-1):
    return jax.nn.softmax(x, axis=axis)

def _gelu(x):
    return jax.nn.gelu(x, approximate=True)

def _silu(x):
    return jax.nn.silu(x)

def _sigmoid(x):
    return jax.nn.sigmoid(x)

def _layernorm(x, axis=-1, eps=1e-05):
    m = jnp.mean(x, axis=axis, keepdims=True)
    v = jnp.var(x, axis=axis, keepdims=True)
    return (x - m) / jnp.sqrt(v + eps)

def _scatter_add(tgt, idx, src, axis=0):
    return tgt.at[idx].add(src)

def _segment_sum(src, seg, n):
    return jax.ops.segment_sum(src, seg, n)
kernel_name = 'mk_adj_preln_d4_adj_r2_fb45a6'

def setup_inputs(seed: int=0):
    np.random.seed(seed)
    _w = jnp.asarray

    def _rec_inputs():
        import jax
        import jax.numpy as jnp
        _gk = jax.random.key(seed)
        x = -0.0005146 + 1 * jax.random.normal(jax.random.fold_in(_gk, 1), (8, 1024, 128), jnp.float32)
        _a = jax.random.bernoulli(jax.random.fold_in(_gk, 2), 0.015625, (8, 1024, 1024))
        _a = jnp.logical_or(_a, jnp.swapaxes(_a, -1, -2))
        _a = jnp.logical_or(_a, jnp.eye(1024, dtype=bool))
        adj = _a.astype(jnp.int32)
        return (x, adj)
    x, adj = _rec_inputs()

    def _L0_gnn_setup():
        import jax, jax.numpy as jnp
        import numpy as np
        B, N, C, OUT, S = (4, 1024, 128, 128, 25)
        DENSITY = 0.008
        key = jax.random.key(seed)
        kA, kX, kW = jax.random.split(key, 3)
        A = jax.random.bernoulli(kA, DENSITY, (B, N, N)).astype(jnp.int32)
        X = jax.random.normal(kX, (B, N, C), dtype=jnp.float32)
        W = jax.random.normal(kW, (2 * C, OUT), dtype=jnp.float32) * np.float32(1.0 / np.sqrt(2 * C))
        b = jnp.zeros((OUT,), dtype=jnp.float32)
        return {'A': A, 'X': X, 'W': W, 'b': b}
    _L0_gnn_all = _L0_gnn_setup()
    _L0_gnn_in = {k: v for k, v in _L0_gnn_all.items() if k in ('W', 'b')}
    del _L0_gnn_all

    def _L1_gnn_setup():
        import jax, jax.numpy as jnp
        import numpy as np
        key = jax.random.key(seed)
        k1, k2, k3, k4 = jax.random.split(key, 4)
        B, N, F, U = (8, 1024, 128, 128)
        x = jax.random.normal(k1, (B, N, F), dtype=jnp.float32)
        adj = jax.random.randint(k2, (B, N, N), 0, 2, dtype=jnp.int32)
        W_msg = jax.random.normal(k3, (F, U), dtype=jnp.float32) / np.sqrt(F)
        W_upd = jax.random.normal(k4, (F, U), dtype=jnp.float32) / np.sqrt(F)
        bias = jnp.zeros((U,), dtype=jnp.float32)
        return {'x': x, 'adj': adj, 'W_msg': W_msg, 'W_upd': W_upd, 'bias': bias}
    _L1_gnn_all = _L1_gnn_setup()
    _L1_gnn_in = {k: v for k, v in _L1_gnn_all.items() if k in ('W_msg', 'W_upd', 'bias')}
    del _L1_gnn_all

    def _L2_gnn_setup():
        import jax, jax.numpy as jnp
        import numpy as np
        ALPHA = 0.2
        key = jax.random.key(seed)
        k1, k2, k3, k4 = jax.random.split(key, 4)
        B, N, F_IN, F_OUT = (4, 2048, 128, 128)
        h = jax.random.normal(k1, (B, N, F_IN), dtype=jnp.float32)
        adj = jax.random.randint(k2, (B, N, N), 0, 2, dtype=jnp.int32)
        std_W = 1.414 * np.sqrt(2.0 / (F_IN + F_OUT))
        W = jax.random.normal(k3, (F_IN, F_OUT), dtype=jnp.float32) * std_W
        std_a = 1.414 * np.sqrt(2.0 / (1 + 2 * F_OUT))
        a = jax.random.normal(k4, (1, 2 * F_OUT), dtype=jnp.float32) * std_a
        return {'h': h, 'adj': adj, 'W': W, 'a': a}
    _L2_gnn_all = _L2_gnn_setup()
    _L2_gnn_in = {k: v for k, v in _L2_gnn_all.items() if k in ('W', 'a')}
    del _L2_gnn_all

    def _L3_gnn_setup():
        import jax, jax.numpy as jnp
        import numpy as np
        NEG_INF = -1000000000.0
        LEAKY_SLOPE = 0.2
        key = jax.random.key(seed)
        k1, k2, k3, k4 = jax.random.split(key, 4)
        B, N, D_in, D_out = (8, 1024, 128, 128)
        x = jax.random.normal(k1, (B, N, D_in), dtype=jnp.float32)
        adj_matrix = jax.random.randint(k2, (B, N, N), 0, 2, dtype=jnp.int32)
        W = jax.random.normal(k3, (D_out, D_in), dtype=jnp.float32) / np.sqrt(D_in)
        a = jax.random.normal(k4, (1, 2 * D_out), dtype=jnp.float32) / np.sqrt(2 * D_out)
        return {'x': x, 'adj_matrix': adj_matrix, 'W': W, 'a': a}
    _L3_gnn_all = _L3_gnn_setup()
    _L3_gnn_in = {k: v for k, v in _L3_gnn_all.items() if k in ('W', 'a')}
    del _L3_gnn_all
    return {'x': x, 'adj': adj, 'L0_gnn_W': _L0_gnn_in['W'], 'L0_gnn_b': _L0_gnn_in['b'], 'L1_gnn_W_msg': _L1_gnn_in['W_msg'], 'L1_gnn_W_upd': _L1_gnn_in['W_upd'], 'L1_gnn_bias': _L1_gnn_in['bias'], 'L2_gnn_W': _L2_gnn_in['W'], 'L2_gnn_a': _L2_gnn_in['a'], 'L3_gnn_W': _L3_gnn_in['W'], 'L3_gnn_a': _L3_gnn_in['a']}

def reference(x, adj, L0_gnn_W, L0_gnn_b, L1_gnn_W_msg, L1_gnn_W_upd, L1_gnn_bias, L2_gnn_W, L2_gnn_a, L3_gnn_W, L3_gnn_a):
    import jax
    import jax.numpy as jnp

    def _L0_gnn_ref(A, X, W, b):
        import jax, jax.numpy as jnp
        import numpy as np
        B, N, C, OUT, S = (4, 1024, 128, 128, 25)
        DENSITY = 0.008
        mask = A != 0
        neg_inf = jnp.float32(-jnp.inf)
        pri = -jnp.arange(N, dtype=jnp.float32)
        scores = jnp.where(mask, pri, neg_inf)
        vals, idx = jax.lax.top_k(scores, S)
        valid = vals > neg_inf
        feats = jax.vmap(lambda x, i: x[i])(X, idx)
        feats = jnp.where(valid[..., None], feats, neg_inf)
        agg = feats.max(axis=2)
        degree = mask.sum(axis=-1)
        agg = jnp.where((degree <= S)[..., None], jnp.maximum(agg, 0.0), agg)
        h = jnp.concatenate([X, agg], axis=-1)
        out = jax.nn.relu(jnp.einsum('bnf,fo->bno', h, W) + b)
        return out

    def _L1_gnn_ref(x, adj, W_msg, W_upd, bias):
        import jax, jax.numpy as jnp
        import numpy as np
        a = adj.astype(x.dtype)
        h = jnp.einsum('bnf,fu->bnu', x, W_msg)
        msg_sum = jnp.einsum('bij,biu->bju', a, h)
        deg = jnp.sum(a, axis=1)
        messages = jnp.where(deg[..., None] > 0, msg_sum / jnp.maximum(deg, 1.0)[..., None], 0.0)
        out = jnp.einsum('bnf,fu->bnu', x, W_upd) + messages + bias
        return jax.nn.relu(out)

    def _L2_gnn_ref(h, adj, W, a):
        import jax, jax.numpy as jnp
        import numpy as np
        ALPHA = 0.2
        F_out = W.shape[1]
        Hh = jnp.einsum('bni,io->bno', h, W)
        a_src = a[0, :F_out]
        a_dst = a[0, F_out:]
        s = jnp.einsum('bno,o->bn', Hh, a_src)
        d = jnp.einsum('bno,o->bn', Hh, a_dst)
        logits = s[:, :, None] + d[:, None, :]
        e = jnp.where(adj != 0, jnp.exp(-jax.nn.leaky_relu(logits, negative_slope=ALPHA)), jnp.zeros((), dtype=Hh.dtype))
        rowsum = jnp.sum(e, axis=-1, keepdims=True)
        rowsum = jnp.where(rowsum == 0.0, 1.0, rowsum)
        h_prime = jnp.einsum('bnm,bmo->bno', e, Hh) / rowsum
        return jax.nn.elu(h_prime)

    def _L3_gnn_ref(x, adj_matrix, W, a):
        import jax, jax.numpy as jnp
        import numpy as np
        NEG_INF = -1000000000.0
        LEAKY_SLOPE = 0.2
        h = jnp.einsum('bnd,od->bno', x, W)
        D = h.shape[-1]
        a_left, a_right = (a[0, :D], a[0, D:])
        e = (h @ a_left)[:, :, None] + (h @ a_right)[:, None, :]
        e = jnp.where(e > 0, e, LEAKY_SLOPE * e)
        e = jnp.where(adj_matrix == 0, NEG_INF, e)
        alpha = jax.nn.softmax(e, axis=-1)
        return jnp.einsum('bij,bjd->bid', alpha, h)
    h = jnp.maximum(_layernorm(x, axis=-1), 0.0)
    x = x + _L0_gnn_ref(adj, h, L0_gnn_W, L0_gnn_b)
    h = jnp.maximum(_layernorm(x, axis=-1), 0.0)
    x = x + _L1_gnn_ref(h, adj, L1_gnn_W_msg, L1_gnn_W_upd, L1_gnn_bias)
    h = jnp.maximum(_layernorm(x, axis=-1), 0.0)
    x = x + _L2_gnn_ref(h, adj, L2_gnn_W, L2_gnn_a)
    h = jnp.maximum(_layernorm(x, axis=-1), 0.0)
    x = x + _L3_gnn_ref(h, adj, L3_gnn_W, L3_gnn_a)
    return x

_drawn_inputs = setup_inputs


def setup_inputs(seed=0):
    import zlib

    import numpy as np

    out = dict(_drawn_inputs(seed))
    spreads = {'L0_gnn_b': (0.0, 0.1), 'L1_gnn_bias': (0.0, 0.1)}
    factors = {'L3_gnn_a': 5.414}
    for name, (base, spread) in spreads.items():
        noise = np.random.default_rng([zlib.crc32(name.encode()), seed]).standard_normal(out[name].shape)
        drawn = base * np.exp(spread * noise) if base else spread * noise
        out[name] = jnp.asarray(drawn.astype(out[name].dtype))
    for name, factor in factors.items():
        out[name] = (out[name] * factor).astype(out[name].dtype)
    return out
```

```python
from contextlib import ExitStack

import numpy as np

import concourse.bass as bass
from concourse import mybir

DT = mybir.dt
ALU = mybir.AluOpType
ACT = mybir.ActivationFunctionType
AX = mybir.AxisListType

B, N, C = 8, 1024, 128
P = 128
T = N // P
S = 25
ROUNDS = (S + 7) // 8
HALF = N // 2
SLOPE = 0.2
EPS = 1e-5
FP8_BIG = 2.0 ** 15
MASK_GAIN = 2.0 ** 85
ROWS = N + 1


def build(nc, x, adj, w0, b0, w1m, w1u, b1, w2, a2, w3, a3, out):
    f32, f16, bf16, i32, u32, fp8 = DT.float32, DT.float16, DT.bfloat16, DT.int32, DT.uint32, DT.float8e5
    V, A_, G = nc.vector, nc.scalar, nc.gpsimd
    x_v = x.rearrange("b (t p) c -> b p t c", p=P)
    out_v = out.rearrange("b (t p) c -> b p t c", p=P)
    adj_v = adj.rearrange("b (t p) m -> b p t m", p=P)
    table = [nc.dram_tensor(f"h0_table{i}", [ROWS, C], f32, kind="Internal").ap() for i in range(2)]

    ctx = ExitStack()
    with ctx:
        def sb(name, shape, dt=f32):
            return ctx.enter_context(nc.sbuf_tensor(name, shape, dt))

        def ps(name, shape, dt=f32):
            return ctx.enter_context(nc.psum_tensor(name, shape, dt))

        def sem(name):
            return ctx.enter_context(nc.semaphore(name))

        part_i = sb("part_i", [P, P], i32)
        col_i = sb("col_i", [P, N], i32)
        part = sb("part", [P, P])
        ident = sb("ident", [P, P])
        ident16 = sb("ident16", [P, P], f16)
        mask_pos = sb("mask_pos", [P, P], bf16)
        mask_neg = sb("mask_neg", [P, P], bf16)
        identb = sb("identb", [P, P], bf16)
        desc = sb("desc", [P, N], f16)
        sel_a = sb("sel_a", [P, P], bf16)
        sel_b = sb("sel_b", [P, P], bf16)
        inv_n = sb("inv_n", [P, P])
        zrow = sb("zrow", [1, C])
        w0_s = sb("w0_s", [P, 2, C])
        w1m_s, w1u_s, w2_s, w3_s = (sb(n, [P, C]) for n in ("w1m_s", "w1u_s", "w2_s", "w3_s"))
        w2t, w3t = sb("w2t", [P, C]), sb("w3t", [P, C])
        a2_s, a3_s = sb("a2_s", [P, 2]), sb("a3_s", [P, 2])
        w2sd, w3sd = sb("w2sd", [P, 2]), sb("w3sd", [P, 2])
        b0_s, b1_s = sb("b0_s", [P, C]), sb("b1_s", [P, C])
        adj_s = [sb(f"adj_s{i}", [P, T, N], f16) for i in range(2)]
        mask = sb("mask", [P, T, N], fp8)
        x_lead = sb("x_lead", [P, T, C])
        x_s = sb("x_s", [P, T, C])
        h0 = [sb(f"h0_{i}", [P, T, C]) for i in range(2)]
        vals = sb("vals", [P, N], f16)
        top = sb("top", [P, 8 * ROUNDS], f16)
        idx = [sb(f"idx{i}", [P, 8 * ROUNDS], u32) for i in range(2)]
        rows = [sb(f"rows{i}", [P, S, C]) for i in range(2)]
        pool = sb("pool", [P, T, C])
        pool_t = sb("pool_t", [P, N])
        h = sb("h", [P, T, C])
        h_t = sb("h_t", [P, N])
        upd = sb("upd", [P, T, C])
        hi, mid, lo = (sb(n, [P, T, C], bf16) for n in ("hi", "mid", "lo"))
        rest = sb("rest", [P, T, C])
        vmat = sb("vmat", [P, T, C + 1])
        att = sb("att", [P, T, C + 1])
        e_s = [sb(f"e_s{i}", [P, T, HALF]) for i in range(2)]
        e_two = [sb(f"e_two{i}", [P, HALF]) for i in range(2)]
        rel = sb("rel", [P, N])
        st = sb("st", [P, T, 6])
        mv = sb("mv", [P, T, 2])
        y0 = sb("y0", [P, T])
        t0 = sb("t0", [P, T])
        var = sb("var", [P, T])
        degsum = sb("degsum", [P, T])
        rdeg = sb("rdeg", [P, T])
        sd = sb("sd", [P, T, 2])
        bias1, bias2 = sb("bias1", [P, T]), sb("bias2", [P, T])
        split3 = sb("split3", [P, T, 3], bf16)
        split6 = sb("split6", [P, T, 6], bf16)
        left = sb("left", [P, T])
        left2 = sb("left2", [P, T])
        row_s = sb("row_s", [P, N], bf16)
        row_r = sb("row_r", [P, N], bf16)
        row_uv = sb("row_uv", [P, N], bf16)
        least = sb("least", [P, 1])
        wmax, zmax, peak, ucol, vcol, empty = (sb(n, [P, T]) for n in
                                               ("wmax", "zmax", "peak", "ucol", "vcol", "empty"))
        rsum = sb("rsum", [P, T])
        mean_s = sb("mean_s", [P, C])

        ps_d = ps("ps_d", [P, N])
        ps_z = ps("ps_z", [P, 2, HALF])
        ps_t = [ps(f"ps_t{i}", [P, N], f16) for i in range(2)]
        ps_zb = ps_z[0:6, 1, :].bitcast(bf16)

        s_w = sem("s_w")
        s_iota = sem("s_iota")
        s_const = sem("s_const")
        s_wt = sem("s_wt")
        s_wc = sem("s_wc")
        s_wsd = sem("s_wsd")
        s_wsc = sem("s_wsc")
        s_zero = sem("s_zero")
        s_xl = sem("s_xl")
        s_xs = sem("s_xs")
        s_adj = [sem(f"s_adj{i}") for i in range(2)]
        s_gate = sem("s_gate")
        s_h0 = sem("s_h0")
        s_tab = sem("s_tab")
        s_idx = sem("s_idx")
        s_rows = [sem(f"s_rows{i}") for i in range(2)]
        s_pool = sem("s_pool")
        s_pt = sem("s_pt")
        s_h0t = sem("s_h0t")
        s_poolt = sem("s_poolt")
        s_p0 = sem("s_p0")
        s_x0 = sem("s_x0")
        s_h = sem("s_h")
        s_ht = sem("s_ht")
        s_htc = sem("s_htc")
        s_hm = sem("s_hm")
        s_up = sem("s_up")
        s_hi, s_rest, s_mid, s_lo = sem("s_hi"), sem("s_rest"), sem("s_mid"), sem("s_lo")
        s_upd = sem("s_upd")
        s_msg = sem("s_msg")
        s_x1 = sem("s_x1")
        s_tr = sem("s_tr")
        s_mask = sem("s_mask")
        s_pv = sem("s_pv")
        s_vm = sem("s_vm")
        s_sp = sem("s_sp")
        s_spt = sem("s_spt")
        s_row = sem("s_row")
        s_rb = sem("s_rb")
        s_rel = sem("s_rel")
        s_peak = sem("s_peak")
        s_z = sem("s_z")
        s_e = sem("s_e")
        s_em = sem("s_em")
        s_o = sem("s_o")
        s_oc = sem("s_oc")
        s_neg = sem("s_neg")
        s_exp = sem("s_exp")
        s_mean, s_meanc = sem("s_mean"), sem("s_meanc")
        s_y = sem("s_y")
        s_out = sem("s_out")
        s_chain = sem("s_chain")
        block = ctx.enter_context(nc.Block())

        def over_graphs(eng, lead0, body, last):
            lead0()
            body(0, 0, None)
            with eng.Fori(0, (B - 2) // 2) as k:
                body(2 * k + 1, 1, 2 * k)
                body(2 * k + 2, 0, 2 * k + 1)
            body(B - 1, 1, B - 2)
            last()

        @block.sync
        def _(sp):
            for dst, src in ((w0_s[:, :, :], w0.rearrange("(k p) c -> p k c", p=P)), (w1m_s[:, :], w1m),
                             (w1u_s[:, :], w1u), (w2_s[:, :], w2), (w3_s[:, :], w3)):
                sp.dma_start(dst, src).then_inc(s_w, 16)
            for dst, src in ((a2_s, a2), (a3_s, a3)):
                sp.dma_start(dst[:, :], src.rearrange("a (k c) -> (a c) k", k=2), allow_slow_non_contiguous=True).then_inc(s_w, 16)
            for dst, src in ((b0_s, b0), (b1_s, b1)):
                sp.dma_start(dst[:, :], src.rearrange("(a c) -> a c", a=1).broadcast_to([P, C])).then_inc(s_w, 16)

            def lead(b):
                sp.wait_ge(s_h0, b)
                sp.dma_start(x_lead[:, :, :], x_v[b]).then_inc(s_xl, 16)

            def put_table(b, par):
                sp.wait_ge(s_h0, b + 1)
                sp.sem_inc(s_gate, 1)
                if not (isinstance(b, int) and b < 2):
                    sp.wait_ge(s_pool, T * (b - 1))
                sp.dma_start(table[par][0:N, :].rearrange("(t p) c -> p t c", p=P), h0[par][:, :, :]).then_inc(s_tab, 16)

            def dense_in(d):
                sp.wait_ge(s_out, 16 * d + 16)
                sp.dma_start(x_s[:, :, :], x_v[d]).then_inc(s_xs, 16)

            def dense_out(d):
                sp.wait_ge(s_y, d + 1)
                sp.dma_start(out_v[d], x_s[:, :, :]).then_inc(s_out, 16)

            def lead0():
                sp.sem_inc(s_out, 16)
                sp.wait_ge(s_const, 1)
                for i in range(2):
                    sp.dma_start(table[i][N:ROWS, :], zrow[:, :]).then_inc(s_zero, 16)
                lead(0)
                put_table(0, 0)

            def body(b, par, d):
                if d is not None:
                    dense_in(d)
                if not (isinstance(b, int) and b == B - 1):
                    lead(b + 1)
                    put_table(b + 1, 1 - par)
                if d is not None:
                    dense_out(d)

            def last():
                dense_in(B - 1)
                dense_out(B - 1)

            over_graphs(sp, lead0, body, last)
            sp.wait_ge(s_out, 16 * B + 16)

        @block.gpsimd
        def _(gp):
            G.iota(part_i[:, :], [[0, P]], base=0, channel_multiplier=1).then_inc(s_iota, 1)
            G.iota(col_i[:, :], [[-1, N]], base=N, channel_multiplier=0).then_inc(s_iota, 1)
            G.memset(ident[:, :], 0.0).then_inc(s_iota, 1)
            gp.wait_ge(s_iota, 3)
            G.affine_select(out=ident[:, :], in_=ident[:, :], compare_op=ALU.not_equal, fill=1.0, base=0,
                            pattern=[[-1, P]], channel_multiplier=1).then_inc(s_iota, 1)

            def gate():
                gp.sem_inc(s_gate, 1)

            def load_adj(b, par):
                gp.dma_start(adj_s[par][:, :, :], adj_v[b]).then_inc(s_adj[par], 16)

            def gather(b, b_par, t):
                slot = t % 2
                gp.wait_ge(s_idx, T * b + t + 1)
                if not (isinstance(b, int) and T * b + t < 2):
                    gp.wait_ge(s_pool, T * b + t - 1)
                gate()
                for r in range(S):
                    gp.indirect_dma_start(rows[slot][:, r, :], None, table[b_par],
                                          bass.IndirectOffsetOnAxis(ap=idx[slot][:, r:r + 1], axis=0))\
                      .then_inc(s_rows[slot], 16)

            def body(b, par, d):
                gp.wait_ge(s_tab, 16 * b + 16)
                gate()
                for t in range(T):
                    gather(b, par, t)
                    if t == T - 2 and not (isinstance(b, int) and b == B - 1):
                        if d is not None:
                            gp.wait_ge(s_peak, d + 1)
                            gate()
                        load_adj(b + 1, 1 - par)

            def lead0():
                load_adj(0, 0)
                gp.wait_ge(s_zero, 32)

            over_graphs(gp, lead0, body, lambda: None)

        @block.scalar
        def _(act):
            act.wait_ge(s_wt, 2)
            A_.activation(w2t[:, :], ps_d[:, 0:P], ACT.Copy).then_inc(s_wc, 1)
            A_.activation(w3t[:, :], ps_d[:, P:2 * P], ACT.Copy).then_inc(s_wc, 1)
            act.wait_ge(s_wsd, 2)
            A_.activation(w2sd[:, :], ps_d[:, 0:2], ACT.Copy).then_inc(s_wsc, 1)
            A_.activation(w3sd[:, :], ps_d[:, 2:4], ACT.Copy).then_inc(s_wsc, 1)

            def masks(d):
                for m in range(T):
                    act.wait_ge(s_tr, T * d + m + 1)
                    act.sem_inc(s_gate, 1)
                    A_.activation(mask[:, m, :], ps_t[m % 2][:, :], ACT.Copy, scale=FP8_BIG, bias=-FP8_BIG, saturate=False,
                                  accum_out=degsum[:, m:m + 1]).then_inc(s_mask, 1)

            def relu_t(d, layer):
                act.wait_ge(s_ht, 3 * d + layer)
                A_.activation(h_t[:, :], ps_d[:, :], ACT.Relu).then_inc(s_htc, 1)

            def rows_of(n, value, row, count):
                act.wait_ge(s_spt, value)
                A_.activation(row[0:n, :], ps_zb[0:n, :], ACT.Copy).then_inc(s_row, 1)

            def vmats(d, layer):
                act.wait_ge(s_pv, 2 * d + layer - 1)
                A_.activation(vmat[:, :, 0:C], ps_d[:, :].rearrange("p (t c) -> p t c", t=T), ACT.Copy)\
                  .then_inc(s_vm, 1)

            def exps(d, layer, half, m):
                one = layer == 2
                u = half * T + m
                zbase = 48 * d + (0 if one else 16)
                ebase = 48 * d + (0 if one else 16)
                tile = 32 * d + (0 if one else 16) + u
                slot = u % 2
                k1, k2 = (-1.0, -SLOPE) if one else (1.0, 1.0)
                act.wait_ge(s_z, zbase + (u + 1 if one else 2 * u + 1))
                A_.activation(e_s[half][:, m, :], ps_z[:, slot if one else 0, :], ACT.Exp, scale=k1,
                              bias=bias1[:, m:m + 1]).then_inc(s_e, 1)
                if not one:
                    act.wait_ge(s_z, zbase + 2 * u + 2)
                if u >= 2:
                    act.wait_ge(s_em, tile - 1)
                A_.activation(e_two[slot][:, :], ps_z[:, slot if one else 1, :], ACT.Exp, scale=k2,
                              bias=bias2[:, m:m + 1]).then_inc(s_e, 1)

            def sums(d, layer, half):
                for n in range(T // 2):
                    q = half * (T // 2) + n
                    act.wait_ge(s_o, 16 * d + (layer - 2) * 8 + q + 1)
                    A_.activation(att[:, q, :], ps_d[:, (q % 2) * HALF:(q % 2) * HALF + C + 1], ACT.Copy)\
                      .then_inc(s_oc, 1)

            def attention(d, layer):
                for m in range(T):
                    exps(d, layer, 0, m)
                for m in range(T):
                    exps(d, layer, 1, m)
                    if m % 2 == 1:
                        n = m // 2
                        act.wait_ge(s_o, 16 * d + (layer - 2) * 8 + n + 1)
                        A_.activation(att[:, n, :], ps_d[:, (n % 2) * HALF:(n % 2) * HALF + C + 1], ACT.Copy)\
                          .then_inc(s_oc, 1)
                sums(d, layer, 1)

            def dense(d):
                act.wait_ge(s_pt, d + 1)
                A_.activation(h_t[:, :], ps_d[:, :], ACT.Copy).then_inc(s_h0t, 1)
                masks(d)
                relu_t(d, 1)
                act.wait_ge(s_hm, d + 1)
                A_.activation(hi[:, :, :], ps_z[:, :, :], ACT.Copy).then_inc(s_hi, 1)
                act.wait_ge(s_rest, d + 1)
                A_.activation(mid[:, :, :], rest[:, :, :], ACT.Copy).then_inc(s_mid, 1)
                relu_t(d, 2)
                vmats(d, 2)
                rows_of(3, 3 * d + 1, row_s, 3)
                attention(d, 2)
                act.wait_ge(s_neg, d + 1)
                A_.activation(upd[:, :, :], upd[:, :, :], ACT.Exp).then_inc(s_exp, 1)
                relu_t(d, 3)
                vmats(d, 3)
                rows_of(3, 3 * d + 2, row_r, 3)
                rows_of(6, 3 * d + 3, row_uv, 6)
                attention(d, 3)
                act.wait_ge(s_mean, d + 1)
                A_.activation(mean_s[:, :], ps_d[:, 0:C], ACT.Copy).then_inc(s_meanc, 1)

            def body(b, par, d):
                if d is not None:
                    dense(d)

            over_graphs(act, lambda: None, body, lambda: dense(B - 1))

        @block.vector
        def _(dve):
            done = [0]

            def mark(ins):
                ins.then_inc(s_chain, 1)
                done[0] += 1

            def step(ins):
                mark(ins)
                dve.wait_ge(s_chain, done[0])

            def clear():
                dve.wait_ge(s_chain, done[0])
                dve.sem_clear(s_chain)
                done[0] = 0

            dve.wait_ge(s_iota, 4)
            mark(V.memset(zrow[:, :], 0.0))
            mark(V.memset(inv_n[:, :], 1.0 / N))
            mark(V.memset(vmat[:, :, C:C + 1], 1.0))
            for row in (row_s, row_r, row_uv):
                mark(V.memset(row[:, :], 0.0))
            mark(V.tensor_copy(part[:, :], part_i[:, :]))
            mark(V.tensor_copy(desc[:, :], col_i[:, :]))
            mark(V.tensor_copy(ident16[:, :], ident[:, :]))
            mark(V.tensor_copy(identb[:, :], ident[:, :]))
            mark(V.tensor_scalar(mask_pos[:, :], ident[:, :], MASK_GAIN, None, ALU.mult))
            mark(V.tensor_scalar(mask_neg[:, :], ident[:, :], -MASK_GAIN, None, ALU.mult))
            dve.wait_ge(s_chain, done[0])
            mark(V.tensor_scalar(sel_a[:, :], part[:, :], 3.0, None, ALU.is_lt))
            step(V.tensor_scalar(sel_b[:, :], part[:, :], 3.0, None, ALU.is_ge))
            step(V.scalar_tensor_tensor(sel_b[:, :], part[:, :], 6.0, sel_b[:, :], ALU.is_lt, ALU.mult))
            V.memset(left[:, :], 0.0).then_inc(s_const, 1)
            dve.wait_ge(s_w, 16 * 9)

            def norm(src, dst):
                for t in range(T):
                    mark(V.bn_stats(st[:, t, :], src[:, t, :]))
                dve.wait_ge(s_chain, done[0])
                for t in range(T):
                    mark(V.bn_aggr(mv[:, t, :], st[:, t, :]))
                dve.wait_ge(s_chain, done[0])
                step(V.tensor_scalar(var[:, :], mv[:, :, 1], EPS, None, ALU.add))
                step(V.tensor_scalar(y0[:, :].bitcast(i32), var[:, :].bitcast(i32), -0.5, 1597463007.0, ALU.mult, ALU.add))
                for _ in range(3):
                    step(V.scalar_tensor_tensor(t0[:, :], y0[:, :], -0.5, y0[:, :], ALU.mult, ALU.mult))
                    step(V.tensor_tensor(t0[:, :], t0[:, :], var[:, :], ALU.mult))
                    step(V.scalar_tensor_tensor(y0[:, :], t0[:, :], 1.5, y0[:, :], ALU.add, ALU.mult))
                for t in range(T - 1):
                    mark(V.tensor_scalar(dst[:, t, :], src[:, t, :], mv[:, t, 0:1], y0[:, t:t + 1],
                                         ALU.subtract, ALU.mult))
                t = T - 1
                return V.tensor_scalar(dst[:, t, :], src[:, t, :], mv[:, t, 0:1], y0[:, t:t + 1],
                                       ALU.subtract, ALU.mult)

            def lead(b, par):
                dve.wait_ge(s_xl, 16 * b + 16)
                step(norm(x_lead, h0[par]))
                V.tensor_scalar(h0[par][:, :, :], h0[par][:, :, :], 0.0, None, ALU.max).then_inc(s_h0, 1)

            def indices(b, par, t):
                if t == 0:
                    dve.wait_ge(s_adj[par], (b // 2 + 1) * 16 if isinstance(b, int) else (b - par) * 8 + 16)
                dve.wait_ge(s_rows[t % 2], 16 * S * (T // 2 * b + t // 2))
                step(V.tensor_tensor(vals[:, :], adj_s[par][:, t, :], desc[:, :], ALU.mult))
                for r in range(ROUNDS):
                    step(V.max(top[:, 8 * r:8 * r + 8], vals[:, :]))
                    if r < ROUNDS - 1:
                        step(V.match_replace(vals[:, :], top[:, 8 * r:8 * r + 8], vals[:, :], 0.0))
                V.tensor_scalar(idx[t % 2][:, :], top[:, :], -1.0, float(N), ALU.mult, ALU.add).then_inc(s_idx, 1)

            def pooled(b, t):
                dve.wait_ge(s_rows[t % 2], 16 * S * (T // 2 * b + t // 2 + 1))
                V.tensor_reduce(pool[:, t, :], rows[t % 2][:, :, :].rearrange("p r c -> p c r"), AX.X, ALU.max)\
                 .then_inc(s_pool, 1)

            def layer0(d):
                dve.wait_ge(s_pt, d + 1)
                V.tensor_copy(pool_t[:, :], ps_z[:, :, :]).then_inc(s_poolt, 1)
                dve.wait_ge(s_p0, d + 1)
                step(V.tensor_tensor(upd[:, :, :], ps_d[:, :].rearrange("p (t c) -> p t c", t=T),
                                     b0_s[:, None, :].broadcast_to([P, T, C]), ALU.add))
                dve.wait_ge(s_xs, 16 * d + 16)
                mark(V.scalar_tensor_tensor(x_s[:, :, :], upd[:, :, :], 0.0, x_s[:, :, :], ALU.max, ALU.add))
                dve.wait_ge(s_chain, done[0])

            def normed(d, layer):
                norm(x_s, h).then_inc(s_h, 1)
                dve.wait_ge(s_chain, done[0])

            def layer1(d):
                dve.wait_ge(s_hi, d + 1)
                V.tensor_tensor(rest[:, :, :], ps_z[:, :, :].rearrange("p a (t c) -> p (a t) c", t=T // 2), hi[:, :, :],
                                ALU.subtract).then_inc(s_rest, 1)
                dve.wait_ge(s_mid, d + 1)
                V.tensor_tensor(lo[:, :, :], rest[:, :, :], mid[:, :, :], ALU.subtract).then_inc(s_lo, 1)
                dve.wait_ge(s_up, d + 1)
                step(V.tensor_tensor(upd[:, :, :], ps_d[:, :].rearrange("p (t c) -> p t c", t=T),
                                     b1_s[:, None, :].broadcast_to([P, T, C]), ALU.add))
                dve.wait_ge(s_mask, T * d + T)
                step(V.tensor_scalar(rdeg[:, :], degsum[:, :], 1.0 / FP8_BIG, float(N), ALU.mult, ALU.add))
                step(V.tensor_scalar(rdeg[:, :], rdeg[:, :], 1.0, None, ALU.max))
                step(V.reciprocal(rdeg[:, :], rdeg[:, :]))
                dve.wait_ge(s_msg, d + 1)
                for t in range(T):
                    mark(V.scalar_tensor_tensor(upd[:, t, :], ps_z[:, t // 4, (t % 4) * C:(t % 4 + 1) * C],
                                                rdeg[:, t:t + 1], upd[:, t, :], ALU.mult, ALU.add))
                dve.wait_ge(s_chain, done[0])
                step(V.scalar_tensor_tensor(x_s[:, :, :], upd[:, :, :], 0.0, x_s[:, :, :], ALU.max, ALU.add))

            def parts(col, dst, at):
                step(V.tensor_copy(dst[:, :, at], col))
                step(V.tensor_tensor(left[:, :], col, dst[:, :, at], ALU.subtract))
                step(V.tensor_copy(dst[:, :, at + 1], left[:, :]))
                return V.tensor_tensor(dst[:, :, at + 2], left[:, :], dst[:, :, at + 1], ALU.subtract)

            def logits(d, layer):
                dve.wait_ge(s_pv, 2 * d + layer - 1)
                step(V.tensor_copy(sd[:, :, :], ps_z[:, 0, 0:2 * T].rearrange("p (t k) -> p t k", k=2)))

            def combine(d, layer):
                for u in range(2 * T):
                    half, m = u // T, u % T
                    dve.wait_ge(s_e, 64 * d + (layer - 2) * 32 + 2 * u + 2)
                    V.tensor_tensor(e_s[half][:, m, :], e_s[half][:, m, :], e_two[u % 2][:, :],
                                    ALU.min if layer == 2 else ALU.max).then_inc(s_em, 1)

            def attended(d, layer):
                dve.wait_ge(s_oc, 16 * d + (layer - 1) * 8)
                if layer == 2:
                    step(V.tensor_scalar(left[:, :], att[:, :, C], 0.0, None, ALU.is_equal))
                    step(V.tensor_tensor(rsum[:, :], att[:, :, C], left[:, :], ALU.add))
                else:
                    step(V.tensor_tensor(rsum[:, :], att[:, :, C], empty[:, :], ALU.add))
                step(V.reciprocal(rsum[:, :], rsum[:, :]))
                step(V.tensor_tensor(att[:, :, 0:C], att[:, :, 0:C],
                                     rsum[:, :, None].broadcast_to([P, T, C]), ALU.mult))

            def layer2_logits(d):
                logits(d, 2)
                mark(V.tensor_scalar(bias1[:, :], sd[:, :, 1], -1.0, None, ALU.mult))
                mark(V.tensor_scalar(bias2[:, :], sd[:, :, 1], -SLOPE, None, ALU.mult))
                parts(sd[:, :, 0], split3, 0).then_inc(s_sp, 1)

            def layer2_end(d):
                attended(d, 2)
                V.tensor_scalar(upd[:, :, :], att[:, :, 0:C], 0.0, None, ALU.min).then_inc(s_neg, 1)
                dve.wait_ge(s_exp, d + 1)
                step(V.scalar_tensor_tensor(upd[:, :, :], att[:, :, 0:C], 0.0, upd[:, :, :], ALU.max, ALU.add))
                step(V.scalar_tensor_tensor(x_s[:, :, :], upd[:, :, :], -1.0, x_s[:, :, :], ALU.add, ALU.add))

            def layer3_peaks(d, par):
                logits(d, 3)
                mark(V.tensor_copy(bias1[:, :], sd[:, :, 1]))
                mark(V.tensor_scalar(bias2[:, :], sd[:, :, 1], SLOPE, None, ALU.mult))
                parts(sd[:, :, 1], split3, 0).then_inc(s_sp, 1)
                dve.wait_ge(s_rb, d + 1)
                step(V.tensor_reduce(least[:, :], ps_d[:, :], AX.X, ALU.min))
                step(V.tensor_scalar(rel[:, :], ps_d[:, :], least[:, 0:1], 1.0, ALU.subtract, ALU.add))
                for t in range(T):
                    mark(V.tensor_tensor_reduce(out=e_s[t // 4][:, 2 * (t % 4):2 * (t % 4) + 2, :], in0=adj_s[par][:, t, :],
                                                in1=rel[:, :], scale=1.0, scalar=0.0, op0=ALU.mult,
                                                op1=ALU.max, accum_out=wmax[:, t:t + 1]))
                dve.wait_ge(s_chain, done[0])
                mark(V.tensor_scalar(empty[:, :], wmax[:, :], 0.5, None, ALU.is_lt))
                step(V.tensor_scalar(zmax[:, :], wmax[:, :], -1.0, least[:, 0:1], ALU.add, ALU.add))
                step(V.tensor_tensor(zmax[:, :], zmax[:, :], sd[:, :, 0], ALU.add))
                step(V.scalar_tensor_tensor(peak[:, :], zmax[:, :], SLOPE, zmax[:, :], ALU.mult, ALU.max))
                mark(V.tensor_tensor(ucol[:, :], sd[:, :, 0], peak[:, :], ALU.subtract))
                V.scalar_tensor_tensor(vcol[:, :], sd[:, :, 0], SLOPE, peak[:, :], ALU.mult, ALU.subtract).then_inc(s_peak, 1)
                dve.wait_ge(s_peak, d + 1)
                dve.wait_ge(s_chain, done[0])
                step(parts(ucol[:, :], split6, 0))
                parts(vcol[:, :], split6, 3).then_inc(s_sp, 1)

            def layer3_end(d):
                attended(d, 3)
                step(V.tensor_tensor(x_s[:, :, :], att[:, :, 0:C], x_s[:, :, :], ALU.add))
                dve.wait_ge(s_meanc, d + 1)
                for t in range(T):
                    i = V.scalar_tensor_tensor(x_s[:, t, :], mean_s[:, :], empty[:, t:t + 1], x_s[:, t, :],
                                               ALU.mult, ALU.add)
                    if t < T - 1:
                        mark(i)
                    else:
                        i.then_inc(s_y, 1)
                dve.wait_ge(s_chain, done[0])

            def body(b, par, d):
                last = isinstance(b, int) and b == B - 1
                if d is None:
                    for t in range(T):
                        if t >= 2:
                            pooled(b, t - 2)
                            indices(b, par, t)
                    pooled(b, T - 2)
                else:
                    layer0(d)
                    normed(d, 1)
                    layer1(d)
                    pooled(b, 0)
                    indices(b, par, 2)
                    normed(d, 2)
                    pooled(b, 1)
                    indices(b, par, 3)
                    layer2_logits(d)
                    combine(d, 2)
                    pooled(b, 2)
                    indices(b, par, 4)
                    layer2_end(d)
                    normed(d, 3)
                    pooled(b, 3)
                    indices(b, par, 5)
                    layer3_peaks(d, 1 - par)
                    pooled(b, 4)
                    indices(b, par, 6)
                    combine(d, 3)
                    pooled(b, 5)
                    indices(b, par, 7)
                    layer3_end(d)
                    pooled(b, 6)
                if not last:
                    lead(b + 1, 1 - par)
                    indices_lead(b + 1, 1 - par, 0)
                pooled(b, T - 1)
                if not last:
                    indices(b + 1, 1 - par, 1)
                clear()

            def indices_lead(b, par, t):
                indices(b, par, t)

            def lead0():
                lead(0, 0)
                indices(0, 0, 0)
                indices(0, 0, 1)
                clear()

            def finish():
                d = B - 1
                layer0(d)
                normed(d, 1)
                layer1(d)
                normed(d, 2)
                layer2_logits(d)
                combine(d, 2)
                layer2_end(d)
                normed(d, 3)
                layer3_peaks(d, 1)
                combine(d, 3)
                layer3_end(d)

            over_graphs(dve, lead0, body, finish)

        @block.tensor
        def _(pe):
            mm = nc.tensor.matmul
            pe.wait_ge(s_w, 16 * 9)
            pe.wait_ge(s_const, 1)
            nc.tensor.transpose(ps_d[:, 0:P], w2_s[:, :], ident[:, :]).then_inc(s_wt, 1)
            nc.tensor.transpose(ps_d[:, P:2 * P], w3_s[:, :], ident[:, :]).then_inc(s_wt, 1)
            pe.wait_ge(s_wc, 2)
            mm(ps_d[:, 0:2], w2t[:, :], a2_s[:, :], start=True, stop=True).then_inc(s_wsd, 1)
            mm(ps_d[:, 2:4], w3_s[:, :], a3_s[:, :], start=True, stop=True).then_inc(s_wsd, 1)
            pe.wait_ge(s_wsc, 2)

            def transposes(src, dst):
                for t in range(T):
                    last = nc.tensor.transpose(dst(t), src[:, t, :], ident[:, :])
                return last

            def to_d(t):
                return ps_d[:, t * P:(t + 1) * P]

            def to_z(t):
                return ps_z[:, t // 4, (t % 4) * P:(t % 4 + 1) * P]

            def layer0(d, par):
                pe.wait_ge(s_pool, T * d + T)
                pe.wait_ge(s_h0, d + 1)
                transposes(h0[par], to_d)
                transposes(pool, to_z).then_inc(s_pt, 1)
                pe.wait_ge(s_h0t, d + 1)
                pe.wait_ge(s_poolt, d + 1)
                for t in range(T):
                    mm(to_d(t), h_t[:, t * P:(t + 1) * P], w0_s[:, 0, :], start=True, stop=False)
                    last = mm(to_d(t), pool_t[:, t * P:(t + 1) * P], w0_s[:, 1, :], start=False, stop=True)
                last.then_inc(s_p0, 1)

            def masks(d, par):
                for m in range(T):
                    if m >= 2:
                        pe.wait_ge(s_mask, T * d + m - 1)
                    for n in range(T):
                        last = nc.tensor.transpose(ps_t[m % 2][:, n * P:(n + 1) * P],
                                                   adj_s[par][:, n, m * P:(m + 1) * P], ident16[:, :])
                    last.then_inc(s_tr, 1)

            def h_transposes(d, layer):
                pe.wait_ge(s_h, 3 * d + layer)
                transposes(h, to_d).then_inc(s_ht, 1)
                pe.wait_ge(s_htc, 3 * d + layer)

            def project(dst, w):
                for t in range(T):
                    last = mm(dst(t), h_t[:, t * P:(t + 1) * P], w, start=True, stop=True)
                return last

            def layer1(d, par):
                h_transposes(d, 1)
                project(to_z, w1m_s[:, :]).then_inc(s_hm, 1)
                project(to_d, w1u_s[:, :]).then_inc(s_up, 1)
                pe.wait_ge(s_lo, d + 1)
                for j in range(T):
                    for i in range(T):
                        for k, part_k in enumerate((hi, mid, lo)):
                            last = mm(to_z(j), adj_s[par][:, i, j * P:(j + 1) * P], part_k[:, i, :],
                                      start=(i == 0 and k == 0), stop=(i == T - 1 and k == 2))
                last.then_inc(s_msg, 1)

            def attention_in(d, layer, w, wsd):
                h_transposes(d, layer)
                for t in range(T):
                    mm(ps_z[:, 0, 2 * t:2 * t + 2], h_t[:, t * P:(t + 1) * P], wsd, start=True, stop=True)
                project(to_d, w).then_inc(s_pv, 1)

            def part_rows(value, split, n):
                pe.wait_ge(s_sp, value)
                for t in range(T):
                    last = nc.tensor.transpose(ps_zb[0:n, t * P:(t + 1) * P], split[:, t, 0:n], identb[:, :])
                last.then_inc(s_spt, 1)
                pe.wait_ge(s_row, value)

            def unit(slot, gain, sel, row, half, m):
                at = slice(half * HALF, (half + 1) * HALF)
                mm(ps_z[:, slot, :], sel[:, :], row[:, at], start=True, stop=False)
                mm(ps_z[:, slot, :], gain[:, :], mask[:, m, at], start=False, stop=True).then_inc(s_z, 1)

            def sums(d, layer, half, n):
                q = half * (T // 2) + n
                if n == 0:
                    pe.wait_ge(s_em, 32 * d + (layer - 2) * 16 + (half + 1) * T)
                o = 16 * d + (layer - 2) * 8 + q
                if q >= 2:
                    pe.wait_ge(s_oc, o - 1)
                for m in range(T):
                    last = mm(ps_d[:, (q % 2) * HALF:(q % 2) * HALF + C + 1], e_s[half][:, m, n * P:(n + 1) * P],
                              vmat[:, m, :], start=(m == 0), stop=(m == T - 1))
                last.then_inc(s_o, 1)

            def layer2(d):
                attention_in(d, 2, w2_s[:, :], w2sd[:, :])
                part_rows(3 * d + 1, split3, 3)
                pe.wait_ge(s_vm, 2 * d + 1)
                for u in range(2 * T):
                    if u >= 2:
                        pe.wait_ge(s_e, 64 * d + 2 * (u - 1))
                    unit(u % 2, mask_neg, sel_a, row_s, u // T, u % T)
                    if u >= T + 1 and u % 2 == 1:
                        sums(d, 2, 0, (u - T) // 2)
                for n in range(T // 2):
                    sums(d, 2, 1, n)

            def layer3(d):
                attention_in(d, 3, w3t[:, :], w3sd[:, :])
                part_rows(3 * d + 2, split3, 3)
                pe.wait_ge(s_vm, 2 * d + 2)
                for half in range(2):
                    last = mm(ps_d[:, half * HALF:(half + 1) * HALF], sel_a[:, :],
                              row_r[:, half * HALF:(half + 1) * HALF], start=True, stop=True)
                last.then_inc(s_rb, 1)
                part_rows(3 * d + 3, split6, 6)
                for u in range(2 * T):
                    e = 64 * d + 32 + 2 * u
                    if u >= 1:
                        pe.wait_ge(s_e, e - 1)
                    unit(0, mask_pos, sel_a, row_uv, u // T, u % T)
                    if u >= 1:
                        pe.wait_ge(s_e, e)
                    unit(1, mask_pos, sel_b, row_uv, u // T, u % T)
                    if u >= T + 1 and u % 2 == 1:
                        sums(d, 3, 0, (u - T) // 2)
                for n in range(T // 2):
                    sums(d, 3, 1, n)
                pe.wait_ge(s_oc, 16 * d + 15)
                for m in range(T):
                    last = mm(ps_d[:, 0:C], inv_n[:, :], vmat[:, m, 0:C], start=(m == 0), stop=(m == T - 1))
                last.then_inc(s_mean, 1)

            def dense(d, par):
                layer0(d, par)
                masks(d, par)
                layer1(d, par)
                layer2(d)
                layer3(d)

            def body(b, par, d):
                if d is not None:
                    dense(d, 1 - par)

            over_graphs(pe, lambda: None, body, lambda: dense(B - 1, 1))


_INS = ["x", "adj", "L0_gnn_W", "L0_gnn_b", "L1_gnn_W_msg", "L1_gnn_W_upd", "L1_gnn_bias", "L2_gnn_W",
        "L2_gnn_a", "L3_gnn_W", "L3_gnn_a"]


def kernel(**inputs):
    import concourse.bacc as bacc
    from concourse.bass_utils import run_bass_kernel_spmd

    nc = bacc.Bacc("TRN2", target_bir_lowering=False, num_devices=1)
    arrays, args = {}, []
    for name in _INS:
        a = np.ascontiguousarray(inputs[name])
        arrays[f"in_{name}"] = a
        args.append(nc.dram_tensor(f"in_{name}", a.shape, DT.from_np(a.dtype), kind="ExternalInput").ap())
    args.append(nc.dram_tensor("out_x", (B, N, C), DT.float32, kind="ExternalOutput").ap())
    build(nc, *args)
    r = run_bass_kernel_spmd(nc, [arrays], core_ids=[0])
    return r.results[0]["out_x"]
```

```python
from contextlib import ExitStack

import numpy as np

import concourse.bass as bass
from concourse import mybir

DT = mybir.dt
ALU = mybir.AluOpType
ACT = mybir.ActivationFunctionType
AX = mybir.AxisListType

B, N, C = 8, 1024, 128
P = 128
T = N // P
S = 25
SLOTS = 22
RANKS = S - SLOTS
SCALE = 4096.0
ROUNDS = (SLOTS + 7) // 8
K8 = 8 * ROUNDS
MEM = 4
Q = N // MEM
PAT = 2 ** MEM
CODE = 128
HALF = N // 2
SLOPE = 0.2
EPS = 1e-5
FP8_BIG = 2.0 ** 15
MASK_GAIN = 2.0 ** 85
ROWS = Q * PAT + 1


PLACES = {"norm3": 2, "peaks": 2, "layer3": 2 * RANKS - 4}


def build(nc, x, adj, w0, b0, w1m, w1u, b1, w2, a2, w3, a3, out):
    f32, f16, bf16, i32, u32, fp8 = DT.float32, DT.float16, DT.bfloat16, DT.int32, DT.uint32, DT.float8e5
    V, A_, G = nc.vector, nc.scalar, nc.gpsimd
    x_v = x.rearrange("b (t p) c -> b p t c", p=P)
    out_v = out.rearrange("b (t p) c -> b p t c", p=P)
    adj_v = adj.rearrange("b (t p) m -> b p t m", p=P)
    table = [nc.dram_tensor(f"h0_table{i}", [ROWS, C], f32, kind="Internal").ap() for i in range(2)]

    ctx = ExitStack()
    with ctx:
        def sb(name, shape, dt=f32):
            return ctx.enter_context(nc.sbuf_tensor(name, shape, dt))

        def ps(name, shape, dt=f32):
            return ctx.enter_context(nc.psum_tensor(name, shape, dt))

        def sem(name):
            return ctx.enter_context(nc.semaphore(name))

        ident = sb("ident", [P, P])
        ident16 = sb("ident16", [P, P], f16)
        mask_pos = sb("mask_pos", [P, P], bf16)
        mask_neg = sb("mask_neg", [P, P], bf16)
        identb = sb("identb", [P, P], bf16)
        group = sb("group", [P, Q], f16)
        weigh = sb("weigh", [P, 32], f16)
        keep = sb("keep", [P, T, K8])
        sel_a = sb("sel_a", [P, P], bf16)
        sel_b = sb("sel_b", [P, P], bf16)
        inv_n = sb("inv_n", [P, P])
        w0_s = sb("w0_s", [P, 2, C])
        w1m_s, w1u_s, w2_s = (sb(n, [P, C]) for n in ("w1m_s", "w1u_s", "w2_s"))
        w3t = sb("w3t", [P, C])
        a2_s, a3_s = sb("a2_s", [P, 2]), sb("a3_s", [P, 2])
        w2sd, w3sd = sb("w2sd", [P, 2]), sb("w3sd", [P, 2])
        b0_s, b1_s = sb("b0_s", [P, C]), sb("b1_s", [P, C])
        adj_s = sb("adj_s", [P, T, N], f16)
        adj_l = sb("adj_l", [P, 4, N], f16)
        adj_t = [sb(f"adj_t{i}", [P, T, N], f16) for i in range(2)]
        mask = [sb(f"mask{i}", [P, T, N], fp8) for i in range(2)]
        x_lead = sb("x_lead", [P, T, C])
        x_s = sb("x_s", [P, T, C])
        subsets = sb("subsets", [P, PAT, C])
        code_s = [sb(f"code_s{i}", [P, Q]) for i in range(2)]
        code = sb("code", [P, Q])
        top = sb("top", [P, T, K8])
        topi = sb("topi", [P, T, K8], i32)
        idx = [sb(f"idx{i}", [P, T, K8], u32) for i in range(2)]
        rows = [sb(f"rows{i}", [P, SLOTS, C]) for i in range(2)]
        pool = sb("pool", [P, T, C])
        one_hot = [sb(f"one_hot{i}", [P, T, HALF], f16) for i in range(2)]
        h0_hi, h0_lo = sb("h0_hi", [P, T, C], f16), sb("h0_lo", [P, T, C], f16)
        picked = sb("picked", [P, N])
        ones16 = sb("ones16", [P, P], f16)
        upper = sb("upper", [P, P], f16)
        h = sb("h", [P, T, C])
        h_t = sb("h_t", [P, N])
        vmat = sb("vmat", [P, T, C + 1])
        att = sb("att", [P, T, C + 1])
        e_s = [sb(f"e_s{i}", [P, T, HALF]) for i in range(2)]
        e_two = sb("e_two", [P, 2, HALF])
        rel = e_two[:, :, :].rearrange("p a n -> p (a n)")

        def in_e(i, k, dt=f32):
            flat = e_s[i][:, :, :].rearrange("p t n -> p (t n)").bitcast(dt)
            return flat[:, k * N:(k + 1) * N].rearrange("p (t c) -> p t c", t=T)

        setup = in_e(1, 3).rearrange("p t c -> p (t c)")
        w3_s = setup[:, 7 * P:8 * P]
        w2t = in_e(1, 2)[:, 0, :]
        weigh_f = in_e(1, 2)[:, 1, 0:32]
        zrow = in_e(1, 2)[0:1, 2, :]
        part, upper_f, member = (setup[:, k * P:(k + 1) * P] for k in range(3))
        part_i, member_i = (setup[:, k * P:(k + 1) * P].bitcast(i32) for k in (3, 4))
        member, member_i = member[:, 0:32], member_i[:, 0:32]
        group_i = setup[:, 5 * P:5 * P + Q].bitcast(i32)
        h0_d = in_e(0, 0)
        h0_r = in_e(0, 2)
        upto = [in_e(0, j, f16).rearrange("p t c -> p (t c)") for j in range(T)]
        pool_t = in_e(0, 1).rearrange("p t c -> p (t c)")
        upd = in_e(1, 0)
        rest = in_e(1, 1)
        mean_s = upd[:, 0, :]
        hi, mid, lo = (in_e(1, k, bf16) for k in (4, 5, 6))

        def in_h(k):
            flat = h[:, :, :].rearrange("p t c -> p (t c)").bitcast(i32)
            return flat[:, k * T * K8:(k + 1) * T * K8].rearrange("p (t k) -> p t k", t=T)

        subset, count, over, less = (in_h(k) for k in range(4))
        cum = in_h(4).bitcast(f32)
        st = sb("st", [P, T, 6])
        mv = sb("mv", [P, T, 2])
        y0 = sb("y0", [P, T])
        t0 = sb("t0", [P, T])
        var = sb("var", [P, T])
        degsum = [sb(f"degsum{i}", [P, T]) for i in range(2)]
        rdeg = sb("rdeg", [P, T])
        sd = sb("sd", [P, T, 2])
        bias1, bias2 = sb("bias1", [P, T]), sb("bias2", [P, T])
        split3 = sb("split3", [P, T, 3], bf16)
        split6 = sb("split6", [P, T, 6], bf16)
        left = sb("left", [P, T])
        left2 = sb("left2", [P, T])
        row = sb("row", [P, N], bf16)
        least = sb("least", [P, 1])
        wmax, zmax, peak, ucol, vcol, empty = (sb(n, [P, T]) for n in
                                               ("wmax", "zmax", "peak", "ucol", "vcol", "empty"))
        rsum = sb("rsum", [P, T])

        ps_d = ps("ps_d", [P, N])
        ps_z = ps("ps_z", [P, 2, HALF])
        ps_a = ps("ps_a", [P, 2, HALF])
        ps_t = [ps(f"ps_t{i}", [P, N], f16) for i in range(2)]
        ps_zb = ps_z[0:6, 1, :].bitcast(bf16)

        s_w = sem("s_w")
        s_iota = sem("s_iota")
        s_const = sem("s_const")
        s_wt = sem("s_wt")
        s_wc = sem("s_wc")
        s_wsd = sem("s_wsd")
        s_wsc = sem("s_wsc")
        s_zero = sem("s_zero")
        s_xl = sem("s_xl")
        s_xs = sem("s_xs")
        s_adj = sem("s_adj")
        s_lead = [sem(f"s_lead{i}") for i in range(2)]
        s_lt = sem("s_lt")
        s_at = sem("s_at")
        s_code = sem("s_code")
        s_codes = sem("s_codes")
        s_coded = sem("s_coded")
        s_h0d = sem("s_h0d")
        s_h0r = sem("s_h0r")
        s_h0hi = sem("s_h0hi")
        s_h0lo = sem("s_h0lo")
        s_upto = sem("s_upto")
        s_cnt = sem("s_cnt")
        s_rank = sem("s_rank")
        s_hot = sem("s_hot")
        s_pick = sem("s_pick")
        s_picked = sem("s_picked")
        s_gate = sem("s_gate")
        s_h0 = sem("s_h0")
        s_tab = sem("s_tab")
        s_idx = sem("s_idx")
        s_rows = [sem(f"s_rows{i}") for i in range(2)]
        s_pool = sem("s_pool")
        s_pt = sem("s_pt")
        s_h0t = sem("s_h0t")
        s_poolt = sem("s_poolt")
        s_p0 = sem("s_p0")
        s_x0 = sem("s_x0")
        s_h = sem("s_h")
        s_ht = sem("s_ht")
        s_htc = sem("s_htc")
        s_hm = sem("s_hm")
        s_up = sem("s_up")
        s_hi, s_rest, s_mid, s_lo = sem("s_hi"), sem("s_rest"), sem("s_mid"), sem("s_lo")
        s_upd = sem("s_upd")
        s_msg = sem("s_msg")
        s_x1 = sem("s_x1")
        s_mask = sem("s_mask")
        s_pv = sem("s_pv")
        s_vm = sem("s_vm")
        s_sp = sem("s_sp")
        s_spt = sem("s_spt")
        s_row = sem("s_row")
        s_rb = sem("s_rb")
        s_rel = sem("s_rel")
        s_peak = sem("s_peak")
        s_z = sem("s_z")
        s_e = sem("s_e")
        s_em = sem("s_em")
        s_o = sem("s_o")
        s_oc = sem("s_oc")
        s_neg = sem("s_neg")
        s_exp = sem("s_exp")
        s_mean, s_meanc = sem("s_mean"), sem("s_meanc")
        s_y = sem("s_y")
        s_out = sem("s_out")
        s_chain = sem("s_chain")
        block = ctx.enter_context(nc.Block())

        units = iter(range(2 * RANKS))
        UNITS_AT = {}
        for place, n in PLACES.items():
            UNITS_AT[place] = [u for _, u in zip(range(n), units)]

        def over_graphs(eng, lead0, body, last):
            lead0()
            body(0, 0, None)
            with eng.Fori(0, (B - 2) // 2) as k:
                body(2 * k + 1, 1, 2 * k)
                body(2 * k + 2, 0, 2 * k + 1)
            body(B - 1, 1, B - 2)
            last()

        @block.sync
        def _(sp):
            for dst, src in ((w0_s[:, :, :], w0.rearrange("(k p) c -> p k c", p=P)), (w1m_s[:, :], w1m),
                             (w1u_s[:, :], w1u), (w2_s[:, :], w2), (w3_s, w3)):
                sp.dma_start(dst, src).then_inc(s_w, 16)
            for dst, src in ((a2_s, a2), (a3_s, a3)):
                sp.dma_start(dst[:, :], src.rearrange("a (k c) -> (a c) k", k=2), allow_slow_non_contiguous=True).then_inc(s_w, 16)
            for dst, src in ((b0_s, b0), (b1_s, b1)):
                sp.dma_start(dst[:, :], src.rearrange("(a c) -> a c", a=1).broadcast_to([P, C])).then_inc(s_w, 16)

            def lead(b):
                sp.wait_ge(s_h0, 2 * b)
                sp.dma_start(x_lead[:, :, :], x[b].rearrange("(p t) c -> p t c", t=T)).then_inc(s_xl, 16)

            def put_table(b, par, g):
                sp.wait_ge(s_h0, 2 * b + g + 1)
                sp.dma_start(table[par][0:Q * PAT, :].rearrange("(p g r) c -> g p (r c)", g=2, r=PAT)[g],
                             subsets[:, :, :]).then_inc(s_tab, 16)

            def h0_back(dst, par, done):
                single = table[par][0:Q * PAT, :].rearrange("(t a r) c -> r a t c", a=P // MEM, r=PAT)
                for m in range(MEM):
                    sp.dma_start(dst[m:P:MEM], single[PAT // 2 >> m]).then_inc(done, 16)

            def dense_in(d):
                sp.wait_ge(s_out, 16 * d + 16)
                sp.dma_start(x_s[:, :, :], x_v[d]).then_inc(s_xs, 16)

            def dense_out(d):
                sp.wait_ge(s_y, d + 1)
                sp.dma_start(out_v[d], x_s[:, :, :]).then_inc(s_out, 16)

            def lead0():
                sp.sem_inc(s_out, 16)
                sp.wait_ge(s_const, 1)
                for i in range(2):
                    sp.dma_start(table[i][Q * PAT:ROWS, :], zrow).then_inc(s_zero, 16)
                lead(0)
                put_table(0, 0, 0)
                put_table(0, 0, 1)

            def body(b, par, d):
                more = not (isinstance(b, int) and b == B - 1)
                if more:
                    lead(b + 1)
                if d is not None:
                    dense_in(d)
                sp.wait_ge(s_tab, 32 * b + 32)
                if not (isinstance(b, int) and b == 0):
                    sp.wait_ge(s_p0, b)
                h0_back(h0_r, par, s_h0r)
                if more:
                    put_table(b + 1, 1 - par, 0)
                if d is not None:
                    sp.wait_ge(s_o, 16 * d + 12)
                else:
                    sp.wait_ge(s_cnt, 2 * T * b + 2 * T)
                h0_back(h0_d, par, s_h0d)
                if more:
                    put_table(b + 1, 1 - par, 1)
                if d is not None:
                    dense_out(d)

            def last():
                dense_in(B - 1)
                dense_out(B - 1)

            over_graphs(sp, lead0, body, last)
            sp.wait_ge(s_out, 16 * B + 16)

        @block.gpsimd
        def _(gp):
            G.iota(part_i[:, :], [[0, P]], base=0, channel_multiplier=1).then_inc(s_iota, 1)
            G.iota(group_i[:, :], [[-CODE, Q]], base=CODE * Q, channel_multiplier=0).then_inc(s_iota, 1)
            G.iota(member_i[:, :], [[-MEM, 32]], base=0, channel_multiplier=1).then_inc(s_iota, 1)
            G.memset(ident[:, :], 0.0).then_inc(s_iota, 1)
            gp.wait_ge(s_iota, 4)
            G.affine_select(out=ident[:, :], in_=ident[:, :], compare_op=ALU.not_equal, fill=1.0, base=0,
                            pattern=[[-1, P]], channel_multiplier=1).then_inc(s_iota, 1)

            G.memset(upper_f[:, :], 1.0).then_inc(s_iota, 1)
            gp.wait_ge(s_iota, 6)
            G.affine_select(out=upper_f[:, :], in_=upper_f[:, :], compare_op=ALU.not_equal, fill=1.5, base=0,
                            pattern=[[-1, P]], channel_multiplier=1).then_inc(s_iota, 1)
            gp.wait_ge(s_iota, 7)
            G.affine_select(out=upper_f[:, :], in_=upper_f[:, :], compare_op=ALU.is_ge, fill=0.0, base=0,
                            pattern=[[1, P]], channel_multiplier=-1).then_inc(s_iota, 1)

            def gate():
                gp.sem_inc(s_gate, 1)

            def load_pair(b, i):
                gp.dma_start(adj_l[:, i % 2 * 2:i % 2 * 2 + 2, :], adj_v[b][:, 2 * i:2 * i + 2, :])\
                  .then_inc(s_lead[i % 2], 16)

            def gather(b, par, t):
                slot = t % 2
                if not (isinstance(b, int) and T * b + t < 2):
                    gp.wait_ge(s_pool, T * b + t - 1)
                    gate()
                for r in range(SLOTS):
                    gp.indirect_dma_start(rows[slot][:, r, :], None, table[par],
                                          bass.IndirectOffsetOnAxis(ap=idx[par][:, t, r:r + 1], axis=0))\
                      .then_inc(s_rows[slot], 16)

            def pairs(b, i):
                if not (isinstance(b, int) and b == 0 and i < 2):
                    gp.wait_ge(s_lt, T * b + 2 * i - 2)
                    gate()
                load_pair(b, i)

            def body(b, par, d):
                more = not (isinstance(b, int) and b == B - 1)
                if more:
                    pairs(b + 1, 0)
                    pairs(b + 1, 1)
                gp.wait_ge(s_tab, 32 * b + 32)
                gate()
                gp.wait_ge(s_idx, b + 1)
                gate()
                for t in range(T):
                    gather(b, par, t)
                    if more and t in (2, 3):
                        pairs(b + 1, t)
                    if t == 5:
                        if d is not None:
                            gp.wait_ge(s_peak, d + 1)
                            gate()
                        gp.dma_start(adj_s[:, :, :], adj_v[b]).then_inc(s_adj, 16)

            def lead0():
                gp.wait_ge(s_zero, 32)
                for i in range(4):
                    pairs(0, i)

            over_graphs(gp, lead0, body, lambda: None)

        @block.scalar
        def _(act):
            act.wait_ge(s_wt, 2)
            A_.activation(w2t, ps_d[:, 0:P], ACT.Copy).then_inc(s_wc, 1)
            A_.activation(w3t[:, :], ps_d[:, P:2 * P], ACT.Copy).then_inc(s_wc, 1)
            act.wait_ge(s_wsd, 2)
            A_.activation(w2sd[:, :], ps_d[:, 0:2], ACT.Copy).then_inc(s_wsc, 1)
            A_.activation(w3sd[:, :], ps_d[:, 2:4], ACT.Copy).then_inc(s_wsc, 1)

            def lead_tile(b, par, k):
                if k < T:
                    act.wait_ge(s_lt, T * b + k + 1)
                    A_.activation(adj_t[par][:, :, k * P:(k + 1) * P],
                                  ps_t[k % 2][:, :].rearrange("p (j n) -> p j n", j=T), ACT.Copy).then_inc(s_at, 1)
                if k > 0:
                    act.wait_ge(s_code, T * b + k)
                    if k > 2:
                        act.sem_inc(s_gate, 1)
                        act.wait_ge(s_coded, T * b + k - 2)
                    A_.activation(code_s[(k - 1) % 2][:, :], ps_t[(k - 1) % 2][:, :].bitcast(f32)[:, Q:2 * Q],
                                  ACT.Copy).then_inc(s_codes, 1)

            def first_part(b, par):
                act.wait_ge(s_h0r, 64 * b + 64)
                A_.activation(h0_hi[:, :, :], h0_r, ACT.Copy, scale=SCALE).then_inc(s_h0hi, 1)

            def masks(b, par):
                act.wait_ge(s_at, T * b + T)
                act.sem_inc(s_gate, 1)
                for m in range(T):
                    A_.activation(mask[par][:, m, :], adj_t[par][:, m, :], ACT.Copy, scale=FP8_BIG, bias=-FP8_BIG,
                                  saturate=False, accum_out=degsum[par][:, m:m + 1]).then_inc(s_mask, 1)

            def ranks(b, par):
                for j in range(T):
                    act.wait_ge(s_upto, (T - 1) * b + min(j + 1, T - 1))
                    act.wait_ge(s_mask, T * b + j + 1)
                    for half in range(2):
                        act.wait_ge(s_cnt, 2 * T * b + 2 * j + half + 1)
                        A_.activation(adj_t[par][:, j, half * HALF:(half + 1) * HALF], ps_a[:, half, :],
                                      ACT.Copy).then_inc(s_rank, 1)

            def relu_t(d, layer):
                act.wait_ge(s_ht, 3 * d + layer)
                A_.activation(h_t[:, :], ps_d[:, :], ACT.Relu).then_inc(s_htc, 1)

            def rows_of(n, value):
                act.wait_ge(s_spt, value)
                A_.activation(row[0:n, :], ps_zb[0:n, :], ACT.Copy).then_inc(s_row, 1)

            def vmats(d, layer):
                act.wait_ge(s_pv, 2 * d + layer - 1)
                A_.activation(vmat[:, :, 0:C], ps_d[:, :].rearrange("p (t c) -> p t c", t=T), ACT.Copy)\
                  .then_inc(s_vm, 1)

            def exps(d, layer, half, m):
                one = layer == 2
                u = half * T + m
                zbase = 48 * d + (0 if one else 16)
                ebase = 48 * d + (0 if one else 16)
                tile = 32 * d + (0 if one else 16) + u
                slot = u % 2
                k1, k2 = (-1.0, -SLOPE) if one else (1.0, 1.0)
                act.wait_ge(s_z, zbase + (u + 1 if one else 2 * u + 1))
                A_.activation(e_s[half][:, m, :], ps_z[:, slot if one else 0, :], ACT.Exp, scale=k1,
                              bias=bias1[:, m:m + 1]).then_inc(s_e, 1)
                if not one:
                    act.wait_ge(s_z, zbase + 2 * u + 2)
                if u >= 2:
                    act.wait_ge(s_em, tile - 1)
                A_.activation(e_two[:, slot, :], ps_z[:, slot if one else 1, :], ACT.Exp, scale=k2,
                              bias=bias2[:, m:m + 1]).then_inc(s_e, 1)

            def sums(d, layer, half):
                for n in range(T // 2):
                    q = half * (T // 2) + n
                    act.wait_ge(s_o, 16 * d + (layer - 2) * 8 + q + 1)
                    A_.activation(att[:, q, :], ps_d[:, (q % 2) * HALF:(q % 2) * HALF + C + 1], ACT.Copy)\
                      .then_inc(s_oc, 1)

            def attention(d, layer, b, par):
                for m in range(T):
                    exps(d, layer, 0, m)
                    if m in (1, 5) and b is not None and layer == 2:
                        lead_tile(b, par, 3 + m // 4)
                for m in range(T):
                    exps(d, layer, 1, m)
                    if m in (1, 5) and b is not None and layer == 2:
                        lead_tile(b, par, 5 + m // 4)
                    if m % 2 == 1:
                        n = m // 2
                        act.wait_ge(s_o, 16 * d + (layer - 2) * 8 + n + 1)
                        A_.activation(att[:, n, :], ps_d[:, (n % 2) * HALF:(n % 2) * HALF + C + 1], ACT.Copy)\
                          .then_inc(s_oc, 1)
                sums(d, layer, 1)

            def dense(d, b, par, g, gpar):
                act.wait_ge(s_pt, d + 1)
                A_.activation(h_t[:, :], ps_d[:, :], ACT.Copy).then_inc(s_h0t, 1)
                if g is not None:
                    first_part(g, gpar)
                if b is not None:
                    lead_tile(b, par, 0)
                    lead_tile(b, par, 1)
                relu_t(d, 1)
                act.wait_ge(s_hm, d + 1)
                A_.activation(hi[:, :, :], ps_z[:, :, :], ACT.Copy).then_inc(s_hi, 1)
                act.wait_ge(s_rest, d + 1)
                A_.activation(mid[:, :, :], rest[:, :, :], ACT.Copy).then_inc(s_mid, 1)
                if b is not None:
                    lead_tile(b, par, 2)
                if g is not None:
                    masks(g, gpar)
                    ranks(g, gpar)
                relu_t(d, 2)
                vmats(d, 2)
                rows_of(3, 3 * d + 1)
                attention(d, 2, b, par)
                if b is not None:
                    lead_tile(b, par, 7)
                act.wait_ge(s_neg, d + 1)
                A_.activation(upd[:, :, :], upd[:, :, :], ACT.Exp).then_inc(s_exp, 1)
                relu_t(d, 3)
                vmats(d, 3)
                rows_of(3, 3 * d + 2)
                if b is not None:
                    lead_tile(b, par, 8)
                rows_of(6, 3 * d + 3)
                attention(d, 3, b, par)
                act.wait_ge(s_mean, d + 1)
                A_.activation(mean_s, ps_d[:, 0:C], ACT.Copy).then_inc(s_meanc, 1)

            def body(b, par, d):
                more = not (isinstance(b, int) and b == B - 1)
                if d is not None:
                    dense(d, b + 1 if more else None, 1 - par, b, par)
                else:
                    first_part(b, par)
                    masks(b, par)
                    ranks(b, par)
                    for k in range(T + 1):
                        lead_tile(b + 1, 1 - par, k)

            def lead0():
                for k in range(T + 1):
                    lead_tile(0, 0, k)

            over_graphs(act, lead0, body, lambda: dense(B - 1, None, None, None, None))

        @block.vector
        def _(dve):
            done = [0]

            def mark(ins):
                ins.then_inc(s_chain, 1)
                done[0] += 1

            def step(ins):
                mark(ins)
                dve.wait_ge(s_chain, done[0])

            def clear():
                dve.wait_ge(s_chain, done[0])
                dve.sem_clear(s_chain)
                done[0] = 0

            dve.wait_ge(s_iota, 8)
            mark(V.memset(zrow, 0.0))
            mark(V.memset(inv_n[:, :], 1.0 / N))
            mark(V.memset(vmat[:, :, C:C + 1], 1.0))
            mark(V.memset(row[:, :], 0.0))
            mark(V.tensor_copy(part[:, :], part_i[:, :]))
            mark(V.tensor_copy(member[:, :], member_i[:, :]))
            mark(V.tensor_copy(upper[:, :], upper_f[:, :]))
            mark(V.memset(ones16[:, :], 1.0))
            mark(V.memset(keep[:, :, 0:1], 0.0))
            mark(V.memset(keep[:, :, 1:K8], 1.0))
            mark(V.tensor_copy(ident16[:, :], ident[:, :]))
            mark(V.tensor_copy(identb[:, :], ident[:, :]))
            mark(V.tensor_scalar(mask_pos[:, :], ident[:, :], MASK_GAIN, None, ALU.mult))
            mark(V.tensor_scalar(mask_neg[:, :], ident[:, :], -MASK_GAIN, None, ALU.mult))
            dve.wait_ge(s_chain, done[0])
            mark(V.tensor_scalar(sel_a[:, :], part[:, :], 3.0, None, ALU.is_lt))
            mark(V.scalar_tensor_tensor(group[:, :], part[:, :].rearrange("p (a n) -> p a n", a=1).broadcast_to([P, 2, P]), 1.0,
                                        group_i, ALU.is_lt, ALU.mult))
            step(V.tensor_scalar(sel_b[:, :], part[:, :], 3.0, None, ALU.is_ge))
            step(V.tensor_scalar(weigh_f, member[:, :], 0.0, 24.0, ALU.is_equal, ALU.mult))
            for m in range(1, MEM):
                step(V.tensor_scalar(weigh[:, :], member[:, :], float(m), 16.0 + (PAT // 2 >> m), ALU.is_equal, ALU.mult))
                step(V.tensor_tensor(weigh_f, weigh_f, weigh[:, :], ALU.add))
            step(V.tensor_copy(weigh[:, :], weigh_f))
            step(V.scalar_tensor_tensor(sel_b[:, :], part[:, :], 6.0, sel_b[:, :], ALU.is_lt, ALU.mult))
            V.memset(left[:, :], 0.0).then_inc(s_const, 1)
            dve.wait_ge(s_w, 16 * 9)

            def norm(src, dst):
                for t in range(T):
                    mark(V.bn_stats(st[:, t, :], src[:, t, :]))
                dve.wait_ge(s_chain, done[0])
                for t in range(T):
                    mark(V.bn_aggr(mv[:, t, :], st[:, t, :]))
                dve.wait_ge(s_chain, done[0])
                step(V.tensor_scalar(var[:, :], mv[:, :, 1], EPS, None, ALU.add))
                step(V.tensor_scalar(y0[:, :].bitcast(i32), var[:, :].bitcast(i32), -0.5, 1597463007.0, ALU.mult, ALU.add))
                for _ in range(3):
                    step(V.scalar_tensor_tensor(t0[:, :], y0[:, :], -0.5, y0[:, :], ALU.mult, ALU.mult))
                    step(V.tensor_tensor(t0[:, :], t0[:, :], var[:, :], ALU.mult))
                    step(V.scalar_tensor_tensor(y0[:, :], t0[:, :], 1.5, y0[:, :], ALU.add, ALU.mult))
                for t in range(T - 1):
                    mark(V.tensor_scalar(dst[:, t, :], src[:, t, :], mv[:, t, 0:1], y0[:, t:t + 1],
                                         ALU.subtract, ALU.mult))
                t = T - 1
                return V.tensor_scalar(dst[:, t, :], src[:, t, :], mv[:, t, 0:1], y0[:, t:t + 1],
                                       ALU.subtract, ALU.mult)

            def lead_norm(b):
                dve.wait_ge(s_xl, 16 * b + 16)
                step(norm(x_lead, x_lead))

            def lead_subsets(b, g):
                if g == 1 or not (isinstance(b, int) and b == 0):
                    dve.wait_ge(s_tab, 32 * b + 16 * g)
                    dve.sem_inc(s_gate, 1)
                mark(V.memset(subsets[:, 0, :], 0.0))
                for m in range(MEM):
                    mark(V.tensor_scalar(subsets[:, PAT // 2 >> m, :], x_lead[:, MEM * g + m, :], 0.0, None, ALU.max))
                dve.wait_ge(s_chain, done[0])
                step(V.tensor_tensor(subsets[:, 3, :], subsets[:, 1, :], subsets[:, 2, :], ALU.max))
                step(V.tensor_tensor(subsets[:, 5:8, :], subsets[:, 1:4, :], subsets[:, 4:5, :].broadcast_to([P, 3, C]),
                                     ALU.max))
                V.tensor_tensor(subsets[:, 9:16, :], subsets[:, 1:8, :], subsets[:, 8:9, :].broadcast_to([P, 7, C]),
                                ALU.max).then_inc(s_h0, 1)

            def tops(b, t):
                dve.wait_ge(s_codes, T * b + t + 1)
                V.scalar_tensor_tensor(code[:, :], ps_t[t % 2][:, :].bitcast(f32)[:, 0:Q], 0.0, code_s[t % 2][:, :],
                                       ALU.is_gt, ALU.mult).then_inc(s_coded, 1)
                dve.wait_ge(s_coded, T * b + t + 1)
                dve.sem_inc(s_gate, 1)
                for r in range(ROUNDS):
                    step(V.max(top[:, t, 8 * r:8 * r + 8], code[:, :]))
                    if r < ROUNDS - 1:
                        step(V.match_replace(code[:, :], top[:, t, 8 * r:8 * r + 8], code[:, :], 0.0))

            def indices(b, par):
                step(V.tensor_copy(topi[:, :, :], top[:, :, :]))
                mark(V.tensor_scalar(subset[:, :, :], topi[:, :, :], PAT - 1, None, ALU.bitwise_and))
                step(V.tensor_scalar(count[:, :, :], topi[:, :, :], 4, 7, ALU.arith_shift_right, ALU.bitwise_and))
                mark(V.tensor_scalar(topi[:, :, :], topi[:, :, :], 3, 0xFFF0, ALU.arith_shift_right, ALU.bitwise_and))
                step(V.tensor_tensor_scan(cum[:, :, :].rearrange("p t k -> p (t k)"), keep[:, :, :].rearrange("p t k -> p (t k)"),
                                          count[:, :, :].rearrange("p t k -> p (t k)"), 0.0, ALU.mult, ALU.add))
                for i in range(1, MEM + 1):
                    step(V.tensor_scalar(over[:, :, :], cum[:, :, :], float(S + i), None, ALU.is_ge))
                    step(V.tensor_tensor(less[:, :, :], subset[:, :, :], over[:, :, :], ALU.subtract))
                    step(V.tensor_tensor(subset[:, :, :], subset[:, :, :], less[:, :, :], ALU.bitwise_and))
                step(V.tensor_scalar(topi[:, :, :], topi[:, :, :], -1.0, float(Q * PAT), ALU.mult, ALU.add))
                if not (isinstance(b, int) and b < 2):
                    dve.wait_ge(s_pool, T * (b - 1))
                V.tensor_tensor(idx[par][:, :, :], topi[:, :, :], subset[:, :, :], ALU.add).then_inc(s_idx, 1)

            def pooled(b, t):
                dve.wait_ge(s_rows[t % 2], 16 * SLOTS * (T // 2 * b + t // 2 + 1))
                V.tensor_reduce(pool[:, t, :], rows[t % 2][:, :, :].rearrange("p r c -> p c r"), AX.X, ALU.max)\
                 .then_inc(s_pool, 1)

            def rest_of_h0(b):
                dve.wait_ge(s_h0hi, b + 1)
                V.scalar_tensor_tensor(h0_lo[:, :, :], h0_r, SCALE, h0_hi[:, :, :], ALU.mult, ALU.subtract)\
                 .then_inc(s_h0lo, 1)

            def sums_upto(b, par):
                dve.wait_ge(s_at, T * b + T)
                for j in range(1, T):
                    if j == 1:
                        V.tensor_copy(upto[1], adj_t[par][:, 0, :]).then_inc(s_upto, 1)
                    else:
                        dve.wait_ge(s_upto, (T - 1) * b + j - 1)
                        V.tensor_tensor(upto[j], upto[j - 1], adj_t[par][:, j - 1, :], ALU.add).then_inc(s_upto, 1)

            def hot(b, par, u):
                rank, half = SLOTS + 1 + u // 2, u % 2
                V.tensor_scalar(one_hot[u % 2][:, :, :], adj_t[par][:, :, half * HALF:(half + 1) * HALF], rank + 0.5,
                                None, ALU.is_equal).then_inc(s_hot, 1)

            def first_hot(b, par):
                dve.wait_ge(s_rank, 2 * T * (b + 1))
                hot(b, par, 0)
                hot(b, par, 1)

            def take(b, par, u):
                half = slice(u % 2 * HALF, (u % 2 + 1) * HALF)
                dve.wait_ge(s_pick, 2 * RANKS * b + u + 1)
                if u < 2:
                    V.tensor_copy(picked[:, half], ps_a[:, u % 2, :]).then_inc(s_picked, 1)
                else:
                    V.tensor_tensor(picked[:, half], picked[:, half], ps_a[:, u % 2, :], ALU.max).then_inc(s_picked, 1)
                if u + 2 < 2 * RANKS:
                    hot(b, par, u + 2)

            def takes(b, par, place):
                for u in UNITS_AT[place]:
                    take(b, par, u)

            def layer0_in(d):
                dve.wait_ge(s_pt, d + 1)
                dve.sem_inc(s_gate, 1)
                dve.wait_ge(s_picked, 2 * RANKS * (d + 1))
                V.scalar_tensor_tensor(pool_t, picked[:, :], 1.0 / SCALE, ps_z[:, :, :].rearrange("p a n -> p (a n)"),
                                       ALU.mult, ALU.max).then_inc(s_poolt, 1)

            def layer0(d):
                dve.wait_ge(s_p0, d + 1)
                step(V.tensor_tensor(upd[:, :, :], ps_d[:, :].rearrange("p (t c) -> p t c", t=T),
                                     b0_s[:, None, :].broadcast_to([P, T, C]), ALU.add))
                dve.wait_ge(s_xs, 16 * d + 16)
                mark(V.scalar_tensor_tensor(x_s[:, :, :], upd[:, :, :], 0.0, x_s[:, :, :], ALU.max, ALU.add))
                dve.wait_ge(s_chain, done[0])

            def normed(d, layer):
                norm(x_s, h).then_inc(s_h, 1)
                dve.wait_ge(s_chain, done[0])

            def message_parts(d):
                dve.wait_ge(s_hi, d + 1)
                V.tensor_tensor(rest[:, :, :], ps_z[:, :, :].rearrange("p a (t c) -> p (a t) c", t=T // 2), hi[:, :, :],
                                ALU.subtract).then_inc(s_rest, 1)
                dve.wait_ge(s_mid, d + 1)
                V.tensor_tensor(lo[:, :, :], rest[:, :, :], mid[:, :, :], ALU.subtract).then_inc(s_lo, 1)

            def layer1(d, par):
                dve.wait_ge(s_up, d + 1)
                step(V.tensor_tensor(upd[:, :, :], ps_d[:, :].rearrange("p (t c) -> p t c", t=T),
                                     b1_s[:, None, :].broadcast_to([P, T, C]), ALU.add))
                dve.wait_ge(s_mask, T * d + T)
                step(V.tensor_scalar(rdeg[:, :], degsum[par][:, :], 1.0 / FP8_BIG, float(N), ALU.mult, ALU.add))
                step(V.tensor_scalar(rdeg[:, :], rdeg[:, :], 1.0, None, ALU.max))
                step(V.reciprocal(rdeg[:, :], rdeg[:, :]))
                dve.wait_ge(s_msg, d + 1)
                for t in range(T):
                    mark(V.scalar_tensor_tensor(upd[:, t, :], ps_z[:, t // 4, (t % 4) * C:(t % 4 + 1) * C],
                                                rdeg[:, t:t + 1], upd[:, t, :], ALU.mult, ALU.add))
                dve.wait_ge(s_chain, done[0])
                step(V.scalar_tensor_tensor(x_s[:, :, :], upd[:, :, :], 0.0, x_s[:, :, :], ALU.max, ALU.add))

            def parts(col, dst, at):
                step(V.tensor_copy(dst[:, :, at], col))
                step(V.tensor_tensor(left[:, :], col, dst[:, :, at], ALU.subtract))
                step(V.tensor_copy(dst[:, :, at + 1], left[:, :]))
                return V.tensor_tensor(dst[:, :, at + 2], left[:, :], dst[:, :, at + 1], ALU.subtract)

            def logits(d, layer):
                dve.wait_ge(s_pv, 2 * d + layer - 1)
                step(V.tensor_copy(sd[:, :, :], ps_z[:, 0, 0:2 * T].rearrange("p (t k) -> p t k", k=2)))

            def combine(d, layer, beside):
                for u in range(2 * T):
                    half, m = u // T, u % T
                    dve.wait_ge(s_e, 64 * d + (layer - 2) * 32 + 2 * u + 2)
                    V.tensor_tensor(e_s[half][:, m, :], e_s[half][:, m, :], e_two[:, u % 2, :],
                                    ALU.min if layer == 2 else ALU.max).then_inc(s_em, 1)
                    beside(u)

            def attended(d, layer):
                dve.wait_ge(s_oc, 16 * d + (layer - 1) * 8)
                if layer == 2:
                    step(V.tensor_scalar(left[:, :], att[:, :, C], 0.0, None, ALU.is_equal))
                    step(V.tensor_tensor(rsum[:, :], att[:, :, C], left[:, :], ALU.add))
                else:
                    step(V.tensor_tensor(rsum[:, :], att[:, :, C], empty[:, :], ALU.add))
                step(V.reciprocal(rsum[:, :], rsum[:, :]))
                step(V.tensor_tensor(att[:, :, 0:C], att[:, :, 0:C],
                                     rsum[:, :, None].broadcast_to([P, T, C]), ALU.mult))

            def layer2_logits(d):
                logits(d, 2)
                mark(V.tensor_scalar(bias1[:, :], sd[:, :, 1], -1.0, None, ALU.mult))
                mark(V.tensor_scalar(bias2[:, :], sd[:, :, 1], -SLOPE, None, ALU.mult))
                parts(sd[:, :, 0], split3, 0).then_inc(s_sp, 1)

            def layer2_end(d):
                attended(d, 2)
                V.tensor_scalar(upd[:, :, :], att[:, :, 0:C], 0.0, None, ALU.min).then_inc(s_neg, 1)
                dve.wait_ge(s_exp, d + 1)
                step(V.scalar_tensor_tensor(upd[:, :, :], att[:, :, 0:C], 0.0, upd[:, :, :], ALU.max, ALU.add))
                step(V.scalar_tensor_tensor(x_s[:, :, :], upd[:, :, :], -1.0, x_s[:, :, :], ALU.add, ALU.add))

            def layer3_peaks(d):
                logits(d, 3)
                mark(V.tensor_copy(bias1[:, :], sd[:, :, 1]))
                mark(V.tensor_scalar(bias2[:, :], sd[:, :, 1], SLOPE, None, ALU.mult))
                parts(sd[:, :, 1], split3, 0).then_inc(s_sp, 1)
                dve.wait_ge(s_rb, d + 1)
                step(V.tensor_reduce(least[:, :], ps_d[:, :], AX.X, ALU.min))
                step(V.tensor_scalar(rel, ps_d[:, :], least[:, 0:1], 1.0, ALU.subtract, ALU.add))
                dve.wait_ge(s_adj, 16 * d + 16)
                for t in range(T):
                    mark(V.tensor_tensor_reduce(out=e_s[t // 4][:, 2 * (t % 4):2 * (t % 4) + 2, :], in0=adj_s[:, t, :],
                                                in1=rel, scale=1.0, scalar=0.0, op0=ALU.mult,
                                                op1=ALU.max, accum_out=wmax[:, t:t + 1]))
                dve.wait_ge(s_chain, done[0])
                mark(V.tensor_scalar(empty[:, :], wmax[:, :], 0.5, None, ALU.is_lt))
                step(V.tensor_scalar(zmax[:, :], wmax[:, :], -1.0, least[:, 0:1], ALU.add, ALU.add))
                step(V.tensor_tensor(zmax[:, :], zmax[:, :], sd[:, :, 0], ALU.add))
                step(V.scalar_tensor_tensor(peak[:, :], zmax[:, :], SLOPE, zmax[:, :], ALU.mult, ALU.max))
                mark(V.tensor_tensor(ucol[:, :], sd[:, :, 0], peak[:, :], ALU.subtract))
                V.scalar_tensor_tensor(vcol[:, :], sd[:, :, 0], SLOPE, peak[:, :], ALU.mult, ALU.subtract).then_inc(s_peak, 1)
                dve.wait_ge(s_peak, d + 1)
                dve.wait_ge(s_chain, done[0])
                step(parts(ucol[:, :], split6, 0))
                parts(vcol[:, :], split6, 3).then_inc(s_sp, 1)

            def layer3_end(d):
                attended(d, 3)
                step(V.tensor_tensor(x_s[:, :, :], att[:, :, 0:C], x_s[:, :, :], ALU.add))
                dve.wait_ge(s_meanc, d + 1)
                for t in range(T):
                    i = V.scalar_tensor_tensor(x_s[:, t, :], mean_s, empty[:, t:t + 1], x_s[:, t, :],
                                               ALU.mult, ALU.add)
                    if t < T - 1:
                        mark(i)
                    else:
                        i.then_inc(s_y, 1)
                dve.wait_ge(s_chain, done[0])

            def body(b, par, d):
                more = not (isinstance(b, int) and b == B - 1)
                nxt = b + 1 if more else None

                def beside2(u):
                    if u == 0:
                        first_hot(b, par)
                    if more and u % 4 == 1:
                        tops(nxt, 2 + u // 4)
                    if u == 6:
                        pooled(b, 2)

                def beside3(u):
                    if u < len(UNITS_AT["peaks"]):
                        take(b, par, UNITS_AT["peaks"][u])
                    if u >= 6 and u % 4 == 2 and u // 4 - 1 < len(UNITS_AT["layer3"]):
                        take(b, par, UNITS_AT["layer3"][u // 4 - 1])
                    if more and u == 3:
                        tops(nxt, T - 1)
                    if u == 5:
                        pooled(b, 5)
                    if more and u == 8:
                        indices(nxt, 1 - par)
                    if more and u == 12:
                        lead_subsets(nxt, 0)

                if d is None:
                    rest_of_h0(b)
                    sums_upto(b, par)
                    first_hot(b, par)
                    for u in range(2 * RANKS):
                        take(b, par, u)
                    lead_norm(nxt)
                    for t in range(T):
                        tops(nxt, t)
                        if t >= 2:
                            pooled(b, t - 2)
                    indices(nxt, 1 - par)
                    lead_subsets(nxt, 0)
                    lead_subsets(nxt, 1)
                    pooled(b, T - 2)
                else:
                    layer0_in(d)
                    if more:
                        lead_norm(nxt)
                    layer0(d)
                    rest_of_h0(b)
                    normed(d, 1)
                    if more:
                        tops(nxt, 0)
                    message_parts(d)
                    if more:
                        tops(nxt, 1)
                    sums_upto(b, par)
                    pooled(b, 0)
                    layer1(d, 1 - par)
                    normed(d, 2)
                    pooled(b, 1)
                    layer2_logits(d)
                    combine(d, 2, beside2)
                    pooled(b, 3)
                    layer2_end(d)
                    normed(d, 3)
                    if more:
                        tops(nxt, 6)
                    takes(b, par, "norm3")
                    pooled(b, 4)
                    layer3_peaks(d)
                    combine(d, 3, beside3)
                    if more:
                        lead_subsets(nxt, 1)
                    pooled(b, 6)
                    layer3_end(d)
                pooled(b, T - 1)
                clear()

            def lead0():
                for t in range(T):
                    tops(0, t)
                indices(0, 0)
                lead_norm(0)
                lead_subsets(0, 0)
                lead_subsets(0, 1)
                clear()

            def finish():
                d = B - 1
                layer0_in(d)
                layer0(d)
                normed(d, 1)
                message_parts(d)
                layer1(d, 1)
                normed(d, 2)
                layer2_logits(d)
                combine(d, 2, lambda u: None)
                layer2_end(d)
                normed(d, 3)
                layer3_peaks(d)
                combine(d, 3, lambda u: None)
                layer3_end(d)

            over_graphs(dve, lead0, body, finish)

        @block.tensor
        def _(pe):
            mm = nc.tensor.matmul
            pe.wait_ge(s_w, 16 * 9)
            pe.wait_ge(s_const, 1)
            nc.tensor.transpose(ps_d[:, 0:P], w2_s[:, :], ident[:, :]).then_inc(s_wt, 1)
            nc.tensor.transpose(ps_d[:, P:2 * P], w3_s, ident[:, :]).then_inc(s_wt, 1)
            pe.wait_ge(s_wc, 2)
            mm(ps_d[:, 0:2], w2t, a2_s[:, :], start=True, stop=True).then_inc(s_wsd, 1)
            mm(ps_d[:, 2:4], w3_s, a3_s[:, :], start=True, stop=True).then_inc(s_wsd, 1)
            pe.wait_ge(s_wsc, 2)

            def transposes(src, dst):
                for t in range(T):
                    last = nc.tensor.transpose(dst(t), src[:, t, :], ident[:, :])
                return last

            def to_d(t):
                return ps_d[:, t * P:(t + 1) * P]

            def to_z(t):
                return ps_z[:, t // 4, (t % 4) * P:(t % 4 + 1) * P]

            def lead_tile(b, par, k):
                if k < T:
                    if k % 2 == 0:
                        i = k // 2
                        pe.wait_ge(s_lead[i % 2], 32 * b + 16 * (i // 2) + 16)
                    if not (isinstance(b, int) and T * b + k < 2):
                        pe.wait_ge(s_coded, T * b + k - 1)
                    for j in range(T):
                        last = nc.tensor.transpose(ps_t[k % 2][:, j * P:(j + 1) * P],
                                                   adj_l[:, k % 4, j * P:(j + 1) * P], ident16[:, :])
                    last.then_inc(s_lt, 1)
                if k > 0:
                    n = k - 1
                    codes = ps_t[n % 2][:, :].bitcast(f32)
                    pe.wait_ge(s_at, T * b + n + 1)
                    for j in range(T):
                        at = adj_t[par][:, j, n * P:(n + 1) * P]
                        mm(codes[:, 32 * j:32 * j + 32], at, weigh[:, :], start=True, stop=True)
                    for j in range(T):
                        at = adj_t[par][:, j, n * P:(n + 1) * P]
                        mm(codes[:, Q + 32 * j:Q + 32 * j + 32], at, weigh[:, :], start=True, stop=False)
                        last = mm(codes[:, Q + 32 * j:Q + 32 * j + 32], ones16[:, :], group[:, 32 * j:32 * j + 32],
                                  start=False, stop=True)
                    last.then_inc(s_code, 1)

            def count(b, par):
                if not (isinstance(b, int) and b == 0):
                    pe.wait_ge(s_picked, 2 * RANKS * b)
                for j in range(T):
                    if j > 0:
                        pe.wait_ge(s_upto, (T - 1) * b + j)
                    for half in range(2):
                        at = slice(half * HALF, (half + 1) * HALF)
                        if j > 0:
                            pe.wait_ge(s_rank, 2 * T * b + 2 * (j - 1) + half + 1)
                        last = mm(ps_a[:, half, :], upper[:, :], adj_t[par][:, j, at], start=True, stop=(j == 0))
                        if j > 0:
                            last = mm(ps_a[:, half, :], ones16[:, :], upto[j][:, at], start=False, stop=True)
                        last.then_inc(s_cnt, 1)

            def pick(b, u, quarters=range(4)):
                for q in quarters:
                    if q == 0:
                        pe.wait_ge(s_hot, 2 * RANKS * b + u + 1)
                        if not (isinstance(b, int) and b == 0 and u < 2):
                            pe.wait_ge(s_picked, 2 * RANKS * b + u - 1)
                    for j in (2 * q, 2 * q + 1):
                        for k, part_k in enumerate((h0_hi, h0_lo)):
                            last = mm(ps_a[:, u % 2, :], part_k[:, j, :], one_hot[u % 2][:, j, :],
                                      start=(j == 0 and k == 0), stop=(j == T - 1 and k == 1))
                    if q == 3:
                        last.then_inc(s_pick, 1)

            def picks(b, place):
                for u in UNITS_AT[place]:
                    pick(b, u)

            def layer0(d, par):
                pe.wait_ge(s_pool, T * d + T)
                pe.wait_ge(s_h0d, 64 * d + 64)
                transposes(h0_d, to_d)
                transposes(pool, to_z).then_inc(s_pt, 1)
                pe.wait_ge(s_h0t, d + 1)
                pe.wait_ge(s_poolt, d + 1)
                for t in range(T):
                    mm(to_d(t), h_t[:, t * P:(t + 1) * P], w0_s[:, 0, :], start=True, stop=False)
                    last = mm(to_d(t), pool_t[:, t * P:(t + 1) * P], w0_s[:, 1, :], start=False, stop=True)
                last.then_inc(s_p0, 1)

            def h_transposes(d, layer):
                pe.wait_ge(s_h, 3 * d + layer)
                transposes(h, to_d).then_inc(s_ht, 1)
                pe.wait_ge(s_htc, 3 * d + layer)

            def project(dst, w):
                for t in range(T):
                    last = mm(dst(t), h_t[:, t * P:(t + 1) * P], w, start=True, stop=True)
                return last

            def layer1_in(d):
                h_transposes(d, 1)
                project(to_z, w1m_s[:, :]).then_inc(s_hm, 1)
                project(to_d, w1u_s[:, :]).then_inc(s_up, 1)

            def layer1(d):
                pe.wait_ge(s_adj, 16 * d + 16)
                pe.wait_ge(s_lo, d + 1)
                for j in range(T):
                    for i in range(T):
                        for k, part_k in enumerate((hi, mid, lo)):
                            last = mm(to_z(j), adj_s[:, i, j * P:(j + 1) * P], part_k[:, i, :],
                                      start=(i == 0 and k == 0), stop=(i == T - 1 and k == 2))
                last.then_inc(s_msg, 1)

            def attention_in(d, layer, w, wsd):
                h_transposes(d, layer)
                for t in range(T):
                    mm(ps_z[:, 0, 2 * t:2 * t + 2], h_t[:, t * P:(t + 1) * P], wsd, start=True, stop=True)
                project(to_d, w).then_inc(s_pv, 1)

            def part_rows(value, split, n):
                pe.wait_ge(s_sp, value)
                for t in range(T):
                    last = nc.tensor.transpose(ps_zb[0:n, t * P:(t + 1) * P], split[:, t, 0:n], identb[:, :])
                last.then_inc(s_spt, 1)
                pe.wait_ge(s_row, value)

            def unit(par, slot, gain, sel, row, half, m):
                at = slice(half * HALF, (half + 1) * HALF)
                mm(ps_z[:, slot, :], sel[:, :], row[:, at], start=True, stop=False)
                mm(ps_z[:, slot, :], gain[:, :], mask[par][:, m, at], start=False, stop=True).then_inc(s_z, 1)

            def sums(d, layer, half, n):
                q = half * (T // 2) + n
                if n == 0:
                    pe.wait_ge(s_em, 32 * d + (layer - 2) * 16 + (half + 1) * T)
                o = 16 * d + (layer - 2) * 8 + q
                if q >= 2:
                    pe.wait_ge(s_oc, o - 1)
                for m in range(T):
                    last = mm(ps_d[:, (q % 2) * HALF:(q % 2) * HALF + C + 1], e_s[half][:, m, n * P:(n + 1) * P],
                              vmat[:, m, :], start=(m == 0), stop=(m == T - 1))
                last.then_inc(s_o, 1)

            def layer2(d, par, b):
                attention_in(d, 2, w2_s[:, :], w2sd[:, :])
                part_rows(3 * d + 1, split3, 3)
                pe.wait_ge(s_vm, 2 * d + 1)
                for u in range(2 * T):
                    if u >= 2:
                        pe.wait_ge(s_e, 64 * d + 2 * (u - 1))
                    unit(par, u % 2, mask_neg, sel_a, row, u // T, u % T)
                    if b is not None and u % 4 == 1:
                        lead_tile(b, par, 3 + u // 4)
                    if u >= T + 1 and u % 2 == 1:
                        sums(d, 2, 0, (u - T) // 2)
                for n in range(T // 2):
                    sums(d, 2, 1, n)

            def layer3(d, par, b, g):
                attention_in(d, 3, w3t[:, :], w3sd[:, :])
                part_rows(3 * d + 2, split3, 3)
                pe.wait_ge(s_vm, 2 * d + 2)
                for half in range(2):
                    last = mm(ps_d[:, half * HALF:(half + 1) * HALF], sel_a[:, :],
                              row[:, half * HALF:(half + 1) * HALF], start=True, stop=True)
                last.then_inc(s_rb, 1)
                if b is not None:
                    lead_tile(b, par, T)
                if g is not None:
                    picks(g, "peaks")
                part_rows(3 * d + 3, split6, 6)
                for u in range(2 * T):
                    e = 64 * d + 32 + 2 * u
                    if u >= 1:
                        pe.wait_ge(s_e, e - 1)
                    unit(par, 0, mask_pos, sel_a, row, u // T, u % T)
                    if u >= 1:
                        pe.wait_ge(s_e, e)
                    unit(par, 1, mask_pos, sel_b, row, u // T, u % T)
                    if g is not None and u >= 2 and (u - 2) // 4 < len(UNITS_AT["layer3"]):
                        pick(g, UNITS_AT["layer3"][(u - 2) // 4], ((u - 2) % 4,))
                    if u >= T + 1 and u % 2 == 1:
                        sums(d, 3, 0, (u - T) // 2)
                for n in range(T // 2):
                    sums(d, 3, 1, n)
                pe.wait_ge(s_oc, 16 * d + 15)
                for m in range(T):
                    last = mm(ps_d[:, 0:C], inv_n[:, :], vmat[:, m, 0:C], start=(m == 0), stop=(m == T - 1))
                last.then_inc(s_mean, 1)

            def dense(d, par, b, g):
                layer0(d, par)
                if b is not None:
                    lead_tile(b, par, 0)
                    lead_tile(b, par, 1)
                layer1_in(d)
                if b is not None:
                    lead_tile(b, par, 2)
                layer1(d)
                if g is not None:
                    count(g, 1 - par)
                layer2(d, par, b)
                if b is not None:
                    lead_tile(b, par, 7)
                if g is not None:
                    picks(g, "norm3")
                layer3(d, par, b, g)

            def body(b, par, d):
                more = not (isinstance(b, int) and b == B - 1)
                if d is not None:
                    dense(d, 1 - par, b + 1 if more else None, b)
                else:
                    count(b, par)
                    for u in range(2 * RANKS):
                        pick(b, u)
                    for k in range(T + 1):
                        lead_tile(b + 1, 1 - par, k)

            def lead0():
                for k in range(T + 1):
                    lead_tile(0, 0, k)

            over_graphs(pe, lead0, body, lambda: dense(B - 1, 1, None, None))


_INS = ["x", "adj", "L0_gnn_W", "L0_gnn_b", "L1_gnn_W_msg", "L1_gnn_W_upd", "L1_gnn_bias", "L2_gnn_W",
        "L2_gnn_a", "L3_gnn_W", "L3_gnn_a"]


def kernel(**inputs):
    import concourse.bacc as bacc
    from concourse.bass_utils import run_bass_kernel_spmd

    nc = bacc.Bacc("TRN2", target_bir_lowering=False, num_devices=1)
    arrays, args = {}, []
    for name in _INS:
        a = np.ascontiguousarray(inputs[name])
        arrays[f"in_{name}"] = a
        args.append(nc.dram_tensor(f"in_{name}", a.shape, DT.from_np(a.dtype), kind="ExternalInput").ap())
    args.append(nc.dram_tensor("out_x", (B, N, C), DT.float32, kind="ExternalOutput").ap())
    build(nc, *args)
    r = run_bass_kernel_spmd(nc, [arrays], core_ids=[0])
    return r.results[0]["out_x"]
```

```python
from contextlib import ExitStack

import numpy as np

import concourse.bass as bass
from concourse import mybir

DT = mybir.dt
ALU = mybir.AluOpType
ACT = mybir.ActivationFunctionType
AX = mybir.AxisListType

B, N, C = 8, 1024, 128
P = 128
T = N // P
S = 25
SLOTS = 21
SLOTS_0 = 13
UNITS = 2 * (S - SLOTS)
UNITS_0 = 2 * (S - SLOTS_0)
PER_TILE_0 = UNITS_0 // T
SCALE = 4096.0
ROUNDS = (SLOTS + 7) // 8
K8 = 8 * ROUNDS
MEM = 4
Q = N // MEM
PAT = 2 ** MEM
CODE = 128
HALF = N // 2
SLOPE = 0.2
EPS = 1e-5
FP8_BIG = 2.0 ** 15
MASK_GAIN = 2.0 ** 85
ROWS = Q * PAT + 1


PLACES = {"layer2": 2, "norm3": 2, "peaks": 2, "layer3": UNITS - 6}
RANKED = 2 * T + 1


def first_graph(b):
    return isinstance(b, int) and b == 0


def slots(b):
    return SLOTS_0 if first_graph(b) else SLOTS


def units(b):
    return UNITS_0 if first_graph(b) else UNITS


def units_before(b):
    return 0 if first_graph(b) else UNITS * b + (UNITS_0 - UNITS)


def rows_until(b, t):
    n = SLOTS * (T // 2 * b + t // 2 + 1)
    return SLOTS_0 * (t // 2 + 1) if first_graph(b) else n - (SLOTS - SLOTS_0) * T // 2


def build(nc, x, adj, w0, b0, w1m, w1u, b1, w2, a2, w3, a3, out):
    f32, f16, bf16, i32, u32, fp8 = DT.float32, DT.float16, DT.bfloat16, DT.int32, DT.uint32, DT.float8e5
    V, A_, G = nc.vector, nc.scalar, nc.gpsimd
    x_v = x.rearrange("b (t p) c -> b p t c", p=P)
    out_v = out.rearrange("b (t p) c -> b p t c", p=P)
    adj_v = adj.rearrange("b (t p) m -> b p t m", p=P)
    table = [nc.dram_tensor(f"h0_table{i}", [ROWS, C], f32, kind="Internal").ap() for i in range(2)]

    ctx = ExitStack()
    with ctx:
        def sb(name, shape, dt=f32):
            return ctx.enter_context(nc.sbuf_tensor(name, shape, dt))

        def ps(name, shape, dt=f32):
            return ctx.enter_context(nc.psum_tensor(name, shape, dt))

        def sem(name):
            return ctx.enter_context(nc.semaphore(name))

        ident = sb("ident", [P, P])
        ident16 = sb("ident16", [P, P], f16)
        mask_pos = sb("mask_pos", [P, P], bf16)
        mask_neg = sb("mask_neg", [P, P], bf16)
        identb = sb("identb", [P, P], bf16)
        group = sb("group", [P, Q], f16)
        weigh = sb("weigh", [P, 32], f16)
        keep = sb("keep", [P, T, K8])
        sel_a = sb("sel_a", [P, P], bf16)
        sel_b = sb("sel_b", [P, P], bf16)
        inv_p = sb("inv_p", [P, P])
        w0_s = sb("w0_s", [P, 2, C])
        w1m_s, w1u_s = (sb(n, [P, C]) for n in ("w1m_s", "w1u_s"))
        w2_s, w3t = sb("w2_s", [P, C + 2]), sb("w3t", [P, C + 2])
        a2_s, a3_s = sb("a2_s", [P, 2]), sb("a3_s", [P, 2])
        w2sd, w3sd = w2_s[:, C:C + 2], w3t[:, C:C + 2]
        b0_s, b1_s = sb("b0_s", [P, C]), sb("b1_s", [P, C])
        adj_s = sb("adj_s", [P, T, N], f16)
        adj_l = sb("adj_l", [P, 4, N], f16)
        adj_t = [sb(f"adj_t{i}", [P, T, N], f16) for i in range(2)]
        mask = [sb(f"mask{i}", [P, T, N], fp8) for i in range(2)]
        x_lead = sb("x_lead", [P, T, C])
        x_s = sb("x_s", [P, T, C])
        subsets = sb("subsets", [P, PAT, C])
        code_s = [sb(f"code_s{i}", [P, Q]) for i in range(2)]
        code = sb("code", [P, Q])
        top = sb("top", [P, T, K8])
        idx = [sb(f"idx{i}", [P, T, K8], u32) for i in range(2)]
        rows = [sb(f"rows{i}", [P, SLOTS, C]) for i in range(2)]
        pool = sb("pool", [P, T, C])
        one_hot = [sb(f"one_hot{i}", [P, T, HALF], f16) for i in range(2)]
        h0_hi, h0_lo = sb("h0_hi", [P, T, C], f16), sb("h0_lo", [P, T, C], f16)
        picked = sb("picked", [P, N])
        ones16 = sb("ones16", [P, P], f16)
        upper = sb("upper", [P, P], f16)
        last_row = sb("last_row", [P, P], f16)
        last_half = sb("last_half", [P, P], f16)
        h = sb("h", [P, T, C])
        h_t = sb("h_t", [P, N])
        vmat = sb("vmat", [P, T, C + 1])
        att = sb("att", [P, T, C + 1])
        e_s = [sb(f"e_s{i}", [P, T, HALF]) for i in range(2)]
        e_two = sb("e_two", [P, 2, HALF])
        e_two4 = [e_two[:, 0, :], e_two[:, 1, :], h_t[:, 0:HALF], h_t[:, HALF:N]]
        rel = e_two[:, :, :].rearrange("p a n -> p (a n)")

        def in_e(i, k, dt=f32):
            flat = e_s[i][:, :, :].rearrange("p t n -> p (t n)").bitcast(dt)
            return flat[:, k * N:(k + 1) * N].rearrange("p (t c) -> p t c", t=T)

        setup = in_e(1, 3).rearrange("p t c -> p (t c)")
        w3_s = setup[:, 7 * P:8 * P]
        w2t = in_e(1, 2)[:, 0, :]
        weigh_f = in_e(1, 2)[:, 1, 0:32]
        zrow = in_e(1, 2)[0:1, 2, :]
        part, upper_f, member = (setup[:, k * P:(k + 1) * P] for k in range(3))
        part_i, member_i = (setup[:, k * P:(k + 1) * P].bitcast(i32) for k in (3, 4))
        member, member_i = member[:, 0:32], member_i[:, 0:32]
        group_i = setup[:, 5 * P:5 * P + Q].bitcast(i32)
        h0_d = in_e(0, 0)
        h0_r = in_e(0, 2)
        x_in = in_e(0, 3)
        rank_0 = in_e(0, 6, f16).rearrange("p t c -> p (t c)")
        pool_t = in_e(0, 1).rearrange("p t c -> p (t c)")
        upd = in_e(1, 0)
        rest = in_e(1, 1)
        neg = in_e(0, 1)
        hi, mid, lo = (in_e(1, k, bf16) for k in (4, 5, 6))

        def in_h(k):
            flat = h[:, :, :].rearrange("p t c -> p (t c)").bitcast(i32)
            return flat[:, k * T * K8:(k + 1) * T * K8].rearrange("p (t k) -> p t k", t=T)

        subset, count, over, topi = (in_h(k) for k in range(4))
        less = count
        cum = in_h(4).bitcast(f32)
        st = sb("st", [P, T, 6])
        mv = sb("mv", [P, T, 2])
        y0, y_lead = sb("y0", [P, T]), sb("y_lead", [P, T])
        my0 = sb("my0", [P, T])
        my_lead = sb("my_lead", [P, T])
        t0 = sb("t0", [P, T])
        var = sb("var", [P, T])
        degsum = [sb(f"degsum{i}", [P, T]) for i in range(2)]
        rdeg = sb("rdeg", [P, T])
        sd = sb("sd", [P, T, 2])
        bias1, bias2 = sb("bias1", [P, T]), sb("bias2", [P, T])
        split3 = sb("split3", [P, T, 3], bf16)
        split6 = sb("split6", [P, T, 6], bf16)
        left = sb("left", [P, T])
        mean_s = sb("mean_s", [P, C])
        row = sb("row", [P, N], bf16)
        least = sb("least", [P, 1])
        wmax, zmax, peak, ucol, vcol, empty = (sb(n, [P, T]) for n in
                                               ("wmax", "zmax", "peak", "ucol", "vcol", "empty"))
        rsum = sb("rsum", [P, T])

        ps_d = ps("ps_d", [P, N])
        ps_z = ps("ps_z", [P, 2, HALF])
        ps_a = ps("ps_a", [P, 2, HALF])
        ps_t = [ps(f"ps_t{i}", [P, N], f16) for i in range(2)]
        pv_d = ps_d[:, :].rearrange("p (a n) -> p a n", a=2)[:, :, 0:2 * (C + 2)].rearrange("p a (k c) -> p a k c", k=2)
        pv_z = ps_z[:, :, 0:2 * (C + 2)].rearrange("p a (k c) -> p a k c", k=2)
        ps_zb = ps_z[0:6, 1, :].bitcast(bf16)

        s_w = sem("s_w")
        s_iota = sem("s_iota")
        s_const = sem("s_const")
        s_wt = sem("s_wt")
        s_wc = sem("s_wc")
        s_wsd = sem("s_wsd")
        s_wsc = sem("s_wsc")
        s_zero = sem("s_zero")
        s_xl = sem("s_xl")
        s_xs = sem("s_xs")
        s_adj = sem("s_adj")
        s_lead = [sem(f"s_lead{i}") for i in range(2)]
        s_lt = sem("s_lt")
        s_at = sem("s_at")
        s_code = sem("s_code")
        s_codes = sem("s_codes")
        s_coded = sem("s_coded")
        s_h0d = sem("s_h0d")
        s_h0r = sem("s_h0r")
        s_h0hi = sem("s_h0hi")
        s_h0lo = sem("s_h0lo")
        s_cnt = sem("s_cnt")
        s_rank = sem("s_rank")
        s_hot = sem("s_hot")
        s_pick = sem("s_pick")
        s_picked = sem("s_picked")
        s_gate = sem("s_gate")
        s_stat = sem("s_stat")
        s_single = sem("s_single")
        s_h0 = sem("s_h0")
        s_tab = sem("s_tab")
        s_idx = sem("s_idx")
        s_rows = [sem(f"s_rows{i}") for i in range(2)]
        s_pool = sem("s_pool")
        s_h0p = sem("s_h0p")
        s_pt = sem("s_pt")
        s_h0t = sem("s_h0t")
        s_poolt = sem("s_poolt")
        s_p0 = sem("s_p0")
        s_h = sem("s_h")
        s_my = sem("s_my")
        s_h2 = sem("s_h2")
        s_ht = sem("s_ht")
        s_htc = sem("s_htc")
        s_hm = sem("s_hm")
        s_up = sem("s_up")
        s_hi, s_rest, s_mid, s_lo = sem("s_hi"), sem("s_rest"), sem("s_mid"), sem("s_lo")
        s_msg = sem("s_msg")
        s_mask = sem("s_mask")
        s_pv = sem("s_pv")
        s_sd = sem("s_sd")
        s_vm = sem("s_vm")
        s_sp = sem("s_sp")
        s_spt = sem("s_spt")
        s_row = sem("s_row")
        s_rb = sem("s_rb")
        s_peak = sem("s_peak")
        s_z = sem("s_z")
        s_e = sem("s_e")
        s_em = sem("s_em")
        s_o = sem("s_o")
        s_oc = sem("s_oc")
        s_neg = sem("s_neg")
        s_exp = sem("s_exp")
        s_mean, s_meanc = sem("s_mean"), sem("s_meanc")
        s_y = sem("s_y")
        s_out = sem("s_out")
        s_chain = sem("s_chain")
        block = ctx.enter_context(nc.Block())

        unit_numbers = iter(range(UNITS))
        UNITS_AT = {}
        for place, n in PLACES.items():
            UNITS_AT[place] = [u for _, u in zip(range(n), unit_numbers)]

        def to_d(t):
            return ps_d[:, t * P:(t + 1) * P]

        def over_graphs(eng, lead0, body, last):
            lead0()
            body(0, 0, None)
            with eng.Fori(0, (B - 2) // 2) as k:
                body(2 * k + 1, 1, 2 * k)
                body(2 * k + 2, 0, 2 * k + 1)
            body(B - 1, 1, B - 2)
            last()

        @block.sync
        def _(sp):
            for dst, src in ((w0_s[:, :, :], w0.rearrange("(k p) c -> p k c", p=P)), (w1m_s[:, :], w1m),
                             (w1u_s[:, :], w1u), (w2_s[:, 0:C], w2), (w3_s, w3)):
                sp.dma_start(dst, src).then_inc(s_w, 16)
            for dst, src in ((a2_s, a2), (a3_s, a3)):
                sp.dma_start(dst[:, :], src.rearrange("a (k c) -> (a c) k", k=2), allow_slow_non_contiguous=True).then_inc(s_w, 16)
            for dst, src in ((b0_s, b0), (b1_s, b1)):
                sp.dma_start(dst[:, :], src.rearrange("(a c) -> a c", a=1).broadcast_to([P, C])).then_inc(s_w, 16)

            def lead(b):
                sp.wait_ge(s_h0, 2 * b)
                sp.dma_start(x_lead[:, :, :], x[b].rearrange("(p t) c -> p t c", t=T)).then_inc(s_xl, 16)

            def put_table(b, par, g):
                sp.wait_ge(s_h0, 2 * b + g + 1)
                sp.dma_start(table[par][0:Q * PAT, :].rearrange("(p g r) c -> g p (r c)", g=2, r=PAT)[g],
                             subsets[:, :, :]).then_inc(s_tab, 16)

            def h0_back(dst, par, done):
                single = table[par][0:Q * PAT, :].rearrange("(t a r) c -> r a t c", a=P // MEM, r=PAT)
                for m in range(MEM):
                    sp.dma_start(dst[m:P:MEM], single[PAT // 2 >> m]).then_inc(done, 16)

            def dense_out(d):
                sp.wait_ge(s_y, d + 1)
                sp.dma_start(out_v[d], x_s[:, :, :]).then_inc(s_out, 16)

            def lead0():
                sp.sem_inc(s_out, 16)
                sp.wait_ge(s_const, 1)
                for i in range(2):
                    sp.dma_start(table[i][Q * PAT:ROWS, :], zrow).then_inc(s_zero, 16)
                lead(0)
                put_table(0, 0, 0)
                put_table(0, 0, 1)

            def body(b, par, d):
                more = not (isinstance(b, int) and b == B - 1)
                if more:
                    lead(b + 1)
                sp.wait_ge(s_tab, 32 * b + 32)
                if not (isinstance(b, int) and b == 0):
                    sp.wait_ge(s_p0, b)
                h0_back(h0_r, par, s_h0r)
                if more:
                    put_table(b + 1, 1 - par, 0)
                    put_table(b + 1, 1 - par, 1)
                if d is not None:
                    sp.wait_ge(s_o, 16 * d + 12)
                else:
                    sp.wait_ge(s_rank, RANKED)
                h0_back(h0_d, par, s_h0d)
                sp.dma_start(x_in, x_v[b]).then_inc(s_xs, 16)
                if d is not None:
                    dense_out(d)

            def last():
                dense_out(B - 1)

            over_graphs(sp, lead0, body, last)
            sp.wait_ge(s_out, 16 * B + 16)

        @block.gpsimd
        def _(gp):
            G.iota(part_i[:, :], [[0, P]], base=0, channel_multiplier=1).then_inc(s_iota, 1)
            G.iota(group_i[:, :], [[-CODE, Q]], base=CODE * Q, channel_multiplier=0).then_inc(s_iota, 1)
            G.iota(member_i[:, :], [[-MEM, 32]], base=0, channel_multiplier=1).then_inc(s_iota, 1)
            G.memset(ident[:, :], 0.0).then_inc(s_iota, 1)
            gp.wait_ge(s_iota, 4)
            G.affine_select(out=ident[:, :], in_=ident[:, :], compare_op=ALU.not_equal, fill=1.0, base=0,
                            pattern=[[-1, P]], channel_multiplier=1).then_inc(s_iota, 1)

            G.memset(upper_f[:, :], 1.0).then_inc(s_iota, 1)
            gp.wait_ge(s_iota, 6)
            G.affine_select(out=upper_f[:, :], in_=upper_f[:, :], compare_op=ALU.not_equal, fill=1.5, base=0,
                            pattern=[[-1, P]], channel_multiplier=1).then_inc(s_iota, 1)
            gp.wait_ge(s_iota, 7)
            G.affine_select(out=upper_f[:, :], in_=upper_f[:, :], compare_op=ALU.is_ge, fill=0.0, base=0,
                            pattern=[[1, P]], channel_multiplier=-1).then_inc(s_iota, 1)

            def gate():
                gp.sem_inc(s_gate, 1)

            def load_pair(b, i):
                gp.dma_start(adj_l[:, i % 2 * 2:i % 2 * 2 + 2, :], adj_v[b][:, 2 * i:2 * i + 2, :])\
                  .then_inc(s_lead[i % 2], 16)

            def gather(b, par, t):
                slot = t % 2
                if not (isinstance(b, int) and T * b + t < 2):
                    gp.wait_ge(s_pool, T * b + t - 1)
                    gate()
                for r in range(slots(b)):
                    gp.indirect_dma_start(rows[slot][:, r, :], None, table[par],
                                          bass.IndirectOffsetOnAxis(ap=idx[par][:, t, r:r + 1], axis=0))\
                      .then_inc(s_rows[slot], 16)

            def pairs(b, i):
                if not (isinstance(b, int) and b == 0 and i < 2):
                    gp.wait_ge(s_lt, T * b + 2 * i - 2)
                    gate()
                load_pair(b, i)

            def body(b, par, d):
                more = not (isinstance(b, int) and b == B - 1)
                if more:
                    pairs(b + 1, 0)
                    pairs(b + 1, 1)
                gp.wait_ge(s_tab, 32 * b + 32)
                gate()
                gp.wait_ge(s_idx, b + 1)
                gate()
                for t in range(T):
                    gather(b, par, t)
                    if more and t in (2, 3):
                        pairs(b + 1, t)
                    if t == 6:
                        if d is not None:
                            gp.wait_ge(s_peak, d + 1)
                            gate()
                        gp.dma_start(adj_s[:, :, :], adj_v[b]).then_inc(s_adj, 16)

            def lead0():
                for i in range(4):
                    pairs(0, i)
                gp.wait_ge(s_zero, 32)

            over_graphs(gp, lead0, body, lambda: None)

        @block.scalar
        def _(act):
            act.wait_ge(s_wt, 2)
            A_.activation(w2t, ps_d[:, 0:P], ACT.Copy).then_inc(s_wc, 1)
            A_.activation(w3t[:, 0:C], ps_d[:, P:2 * P], ACT.Copy).then_inc(s_wc, 1)
            act.wait_ge(s_wsd, 2)
            A_.activation(w2sd, ps_d[:, 0:2], ACT.Copy).then_inc(s_wsc, 1)
            A_.activation(w3sd, ps_d[:, 2:4], ACT.Copy).then_inc(s_wsc, 1)

            def lead_tile(b, par, k):
                if k < T:
                    lead_transposed(b, par, k)
                if k > 0:
                    lead_codes(b, k - 1)

            def lead_transposed(b, par, k):
                act.wait_ge(s_lt, T * b + k + 1)
                A_.activation(adj_t[par][:, :, k * P:(k + 1) * P],
                              ps_t[k % 2][:, :].rearrange("p (j n) -> p j n", j=T), ACT.Copy).then_inc(s_at, 1)
            def lead_codes(b, k):
                act.wait_ge(s_code, T * b + k + 1)
                if k > 1:
                    act.sem_inc(s_gate, 1)
                    act.wait_ge(s_coded, T * b + k - 1)
                A_.activation(code_s[k % 2][:, :], ps_t[k % 2][:, :].bitcast(f32)[:, Q:2 * Q],
                              ACT.Copy).then_inc(s_codes, 1)

            def first_part(b, par):
                act.wait_ge(s_h0r, 64 * b + 64)
                A_.activation(h0_hi[:, :, :], h0_r, ACT.Copy, scale=SCALE).then_inc(s_h0hi, 1)

            def singles(b, g):
                act.wait_ge(s_stat, b + 1)
                if g == 1 or not (isinstance(b, int) and b == 0):
                    act.sem_inc(s_gate, 1)
                    act.wait_ge(s_tab, 32 * b + 16 * g)
                for m in range(MEM):
                    t = MEM * g + m
                    i = A_.activation(subsets[:, PAT // 2 >> m, :], x_lead[:, t, :], ACT.Relu, scale=y_lead[:, t:t + 1],
                                      bias=my_lead[:, t:t + 1])
                i.then_inc(s_single, 1)

            def masks(b, par):
                act.wait_ge(s_at, T * b + T)
                act.sem_inc(s_gate, 1)
                for m in range(T):
                    A_.activation(mask[par][:, m, :], adj_t[par][:, m, :], ACT.Copy, scale=FP8_BIG, bias=-FP8_BIG,
                                  saturate=False, accum_out=degsum[par][:, m:m + 1]).then_inc(s_mask, 1)

            def ranks(b, par):
                for j in range(T):
                    if j > 0:
                        act.wait_ge(s_mask, T * b + j)
                    for half in range(2):
                        at = slice(half * HALF, (half + 1) * HALF)
                        act.wait_ge(s_cnt, 2 * T * b + 2 * j + half + 1)
                        A_.activation(adj_t[par][:, j - 1, at] if j > 0 else rank_0[:, at], ps_a[:, half, :], ACT.Copy)\
                          .then_inc(s_rank, 1)
                act.wait_ge(s_mask, T * b + T)
                act.wait_ge(s_rank, RANKED * b + 2)
                A_.activation(adj_t[par][:, T - 1, :], rank_0, ACT.Copy).then_inc(s_rank, 1)

            def relu_t(d, layer):
                if layer == 3:
                    act.wait_ge(s_my, d + 1)
                    for t in range(T // 2, T):
                        i = A_.activation(h[:, t, :], x_s[:, t, :], ACT.Relu, scale=y0[:, t:t + 1], bias=my0[:, t:t + 1])
                    i.then_inc(s_h2, 1)
                act.wait_ge(s_ht, 3 * d + layer)
                A_.activation(h_t[:, :], ps_d[:, :], ACT.Relu).then_inc(s_htc, 1)

            def rows_of(n, value):
                act.wait_ge(s_spt, value)
                A_.activation(row[0:n, :], ps_zb[0:n, :], ACT.Copy).then_inc(s_row, 1)

            def vmats(d, layer):
                act.wait_ge(s_pv, 2 * d + layer - 1)
                for part, tiles in ((pv_z, sd[:, T // 2:T, :]), (pv_d, sd[:, 0:T // 2, :])):
                    A_.activation(tiles.rearrange("p (a k) c -> p a k c", a=2), part[:, :, :, C:C + 2], ACT.Copy)\
                      .then_inc(s_sd, 1)
                for part, tiles in ((pv_z, vmat[:, T // 2:T, 0:C]), (pv_d, vmat[:, 0:T // 2, 0:C])):
                    A_.activation(tiles.rearrange("p (a k) c -> p a k c", a=2), part[:, :, :, 0:C], ACT.Copy)\
                      .then_inc(s_vm, 1)

            def exps(d, layer, half, m):
                one = layer == 2
                u = half * T + m
                zbase = 48 * d + (0 if one else 16)
                ebase = 48 * d + (0 if one else 16)
                tile = 32 * d + (0 if one else 16) + u
                slot = u % 2
                k1, k2 = (-1.0, -SLOPE) if one else (1.0, 1.0)
                act.wait_ge(s_z, zbase + (u + 1 if one else 2 * u + 1))
                A_.activation(e_s[half][:, m, :], ps_z[:, slot if one else 0, :], ACT.Exp, scale=k1,
                              bias=bias1[:, m:m + 1]).then_inc(s_e, 1)
                if not one:
                    act.wait_ge(s_z, zbase + 2 * u + 2)
                if u >= 4:
                    act.wait_ge(s_em, tile - 3)
                A_.activation(e_two4[u % 4], ps_z[:, slot if one else 1, :], ACT.Exp, scale=k2,
                              bias=bias2[:, m:m + 1]).then_inc(s_e, 1)

            def h0_copied(b):
                act.wait_ge(s_h0p, b + 1)
                A_.activation(h_t[:, :].rearrange("p (a n) -> p a n", a=2), ps_z[:, :, :], ACT.Copy).then_inc(s_h0t, 1)

            def exp_neg(d, half):
                at = slice(half * T // 2, (half + 1) * T // 2)
                act.wait_ge(s_neg, 2 * d + half + 1)
                A_.activation(neg[:, at, :], neg[:, at, :], ACT.Exp).then_inc(s_exp, 1)

            def attention(d, layer, b, par, g):
                for u in range(2 * T):
                    exps(d, layer, u // T, u % T)
                    if layer == 2 and b is not None:
                        if u % 4 == 1:
                            lead_codes(b, 2 + u // 4)
                        if u % 4 == 2:
                            lead_transposed(b, par, 3 + u // 4)
                        if u == 7:
                            singles(b, 1)
                    if u > T and u % 2 == 1:
                        n = (u - T) // 2
                        act.wait_ge(s_o, 16 * d + (layer - 2) * 8 + n + 1)
                        A_.activation(att[:, n, :], ps_d[:, (n % 2) * HALF:(n % 2) * HALF + C + 1], ACT.Copy)\
                          .then_inc(s_oc, 1)
                if layer == 2:
                    exp_neg(d, 0)
                for n in range(T // 2):
                    q = T // 2 + n
                    act.wait_ge(s_o, 16 * d + (layer - 2) * 8 + q + 1)
                    A_.activation(att[:, q, :], ps_d[:, (q % 2) * HALF:(q % 2) * HALF + C + 1], ACT.Copy)\
                      .then_inc(s_oc, 1)
                    if layer == 3 and n == 1 and g is not None:
                        h0_copied(g)

            def dense(d, b, par, g, gpar):
                if g is not None:
                    first_part(g, gpar)
                if b is not None:
                    lead_tile(b, par, 0)
                    lead_tile(b, par, 1)
                relu_t(d, 1)
                act.wait_ge(s_hm, d + 1)
                A_.activation(hi[:, :, :], ps_z[:, :, :], ACT.Copy).then_inc(s_hi, 1)
                act.wait_ge(s_rest, d + 1)
                A_.activation(mid[:, :, :], rest[:, :, :], ACT.Copy).then_inc(s_mid, 1)
                if b is not None:
                    lead_tile(b, par, 2)
                    singles(b, 0)
                if g is not None:
                    masks(g, gpar)
                    ranks(g, gpar)
                relu_t(d, 2)
                vmats(d, 2)
                rows_of(3, 3 * d + 1)
                attention(d, 2, b, par, g)
                if b is not None:
                    lead_tile(b, par, 7)
                exp_neg(d, 1)
                relu_t(d, 3)
                vmats(d, 3)
                rows_of(3, 3 * d + 2)
                act.wait_ge(s_mean, d + 1)
                A_.activation(mean_s[:, :], ps_z[:, 0, 0:C], ACT.Copy, scale=1.0 / T).then_inc(s_meanc, 1)
                if b is not None:
                    lead_tile(b, par, 8)
                rows_of(6, 3 * d + 3)
                attention(d, 3, b, par, g)

            def body(b, par, d):
                more = not (isinstance(b, int) and b == B - 1)
                if d is not None:
                    dense(d, b + 1 if more else None, 1 - par, b, par)
                else:
                    first_part(b, par)
                    masks(b, par)
                    ranks(b, par)
                    for k in range(T + 1):
                        lead_tile(b + 1, 1 - par, k)
                        if k == 3:
                            singles(b + 1, 0)
                        if k == 5:
                            singles(b + 1, 1)
                    h0_copied(b)

            def lead0():
                for k in range(T + 1):
                    lead_tile(0, 0, k)
                    if k == 2:
                        singles(0, 0)
                    if k == 5:
                        singles(0, 1)

            over_graphs(act, lead0, body, lambda: dense(B - 1, None, None, None, None))

        @block.vector
        def _(dve):
            done = [0]

            def mark(ins):
                ins.then_inc(s_chain, 1)
                done[0] += 1

            def step(ins):
                mark(ins)
                dve.wait_ge(s_chain, done[0])

            def clear():
                dve.wait_ge(s_chain, done[0])
                dve.sem_clear(s_chain)
                done[0] = 0

            dve.wait_ge(s_iota, 8)
            mark(V.memset(zrow, 0.0))
            mark(V.memset(inv_p[:, :], 1.0 / P))
            mark(V.memset(vmat[:, :, C:C + 1], 1.0))
            mark(V.memset(row[:, :], 0.0))
            mark(V.tensor_copy(part[:, :], part_i[:, :]))
            mark(V.tensor_copy(member[:, :], member_i[:, :]))
            mark(V.tensor_copy(upper[:, :], upper_f[:, :]))
            mark(V.memset(ones16[:, :], 1.0))
            mark(V.memset(keep[:, :, 0:1], 0.0))
            mark(V.memset(subsets[:, 0, :], 0.0))
            mark(V.memset(keep[:, :, 1:K8], 1.0))
            mark(V.tensor_copy(ident16[:, :], ident[:, :]))
            mark(V.tensor_copy(identb[:, :], ident[:, :]))
            mark(V.tensor_scalar(mask_pos[:, :], ident[:, :], MASK_GAIN, None, ALU.mult))
            mark(V.tensor_scalar(mask_neg[:, :], ident[:, :], -MASK_GAIN, None, ALU.mult))
            dve.wait_ge(s_chain, done[0])
            mark(V.tensor_scalar(last_row[:, :], part[:, :], P - 1.0, None, ALU.is_ge))
            mark(V.tensor_scalar(last_half[:, :], part[:, :], P - 1.0, -0.5, ALU.is_ge, ALU.mult))
            mark(V.tensor_scalar(sel_a[:, :], part[:, :], 3.0, None, ALU.is_lt))
            mark(V.scalar_tensor_tensor(group[:, :], part[:, :].rearrange("p (a n) -> p a n", a=1).broadcast_to([P, 2, P]), 1.0,
                                        group_i, ALU.is_lt, ALU.mult))
            step(V.tensor_scalar(sel_b[:, :], part[:, :], 3.0, None, ALU.is_ge))
            step(V.tensor_scalar(weigh_f, member[:, :], 0.0, 24.0, ALU.is_equal, ALU.mult))
            for m in range(1, MEM):
                step(V.tensor_scalar(weigh[:, :], member[:, :], float(m), 16.0 + (PAT // 2 >> m), ALU.is_equal, ALU.mult))
                step(V.tensor_tensor(weigh_f, weigh_f, weigh[:, :], ALU.add))
            step(V.tensor_copy(weigh[:, :], weigh_f))
            step(V.scalar_tensor_tensor(sel_b[:, :], part[:, :], 6.0, sel_b[:, :], ALU.is_lt, ALU.mult))
            V.memset(left[:, :], 0.0).then_inc(s_const, 1)
            dve.wait_ge(s_w, 16 * 9)

            def stats(src, tiles):
                for t in tiles:
                    mark(V.bn_stats(st[:, t, :], src[:, t, :]))
                dve.wait_ge(s_chain, done[0])
                for t in tiles:
                    mark(V.bn_aggr(mv[:, t, :], st[:, t, :]))

            def rsqrt(y):
                dve.wait_ge(s_chain, done[0])
                step(V.tensor_scalar(var[:, :], mv[:, :, 1], EPS, None, ALU.add))
                step(V.tensor_scalar(y[:, :].bitcast(i32), var[:, :].bitcast(i32), -0.5, 1597463007.0, ALU.mult, ALU.add))
                for _ in range(3):
                    step(V.scalar_tensor_tensor(t0[:, :], y[:, :], -0.5, y[:, :], ALU.mult, ALU.mult))
                    step(V.tensor_tensor(t0[:, :], t0[:, :], var[:, :], ALU.mult))
                    step(V.scalar_tensor_tensor(y[:, :], t0[:, :], 1.5, y[:, :], ALU.add, ALU.mult))

            def lead_stats(b):
                dve.wait_ge(s_xl, 16 * b + 16)
                stats(x_lead, range(T))
                rsqrt(y_lead)
                V.scalar_tensor_tensor(my_lead[:, :], mv[:, :, 0], -1.0, y_lead[:, :], ALU.mult, ALU.mult)\
                 .then_inc(s_stat, 1)
                dve.wait_ge(s_stat, b + 1)
                dve.sem_inc(s_gate, 1)

            def lead_subsets(b, g):
                dve.wait_ge(s_single, 2 * b + g + 1)
                dve.sem_inc(s_gate, 1)
                step(V.tensor_tensor(subsets[:, 3, :], subsets[:, 1, :], subsets[:, 2, :], ALU.max))
                step(V.tensor_tensor(subsets[:, 5:8, :], subsets[:, 1:4, :], subsets[:, 4:5, :].broadcast_to([P, 3, C]),
                                     ALU.max))
                V.tensor_tensor(subsets[:, 9:16, :], subsets[:, 1:8, :], subsets[:, 8:9, :].broadcast_to([P, 7, C]),
                                ALU.max).then_inc(s_h0, 1)

            def tops(b, t):
                dve.wait_ge(s_codes, T * b + t + 1)
                V.scalar_tensor_tensor(code[:, :], ps_t[t % 2][:, :].bitcast(f32)[:, 0:Q], 0.0, code_s[t % 2][:, :],
                                       ALU.is_gt, ALU.mult).then_inc(s_coded, 1)
                dve.wait_ge(s_coded, T * b + t + 1)
                dve.sem_inc(s_gate, 1)
                for r in range(ROUNDS):
                    step(V.max(top[:, t, 8 * r:8 * r + 8], code[:, :]))
                    if r < ROUNDS - 1:
                        step(V.match_replace(code[:, :], top[:, t, 8 * r:8 * r + 8], code[:, :], 0.0))

            def indices(b, par):
                step(V.tensor_copy(topi[:, :, :], top[:, :, :]))
                mark(V.tensor_scalar(subset[:, :, :], topi[:, :, :], PAT - 1, None, ALU.bitwise_and))
                step(V.tensor_scalar(count[:, :, :], topi[:, :, :], 4, 7, ALU.arith_shift_right, ALU.bitwise_and))
                mark(V.tensor_scalar(topi[:, :, :], topi[:, :, :], 3, 0xFFF0, ALU.arith_shift_right, ALU.bitwise_and))
                step(V.tensor_tensor_scan(cum[:, :, :].rearrange("p t k -> p (t k)"), keep[:, :, :].rearrange("p t k -> p (t k)"),
                                          count[:, :, :].rearrange("p t k -> p (t k)"), 0.0, ALU.mult, ALU.add))
                for i in range(1, MEM + 1):
                    step(V.tensor_scalar(over[:, :, :], cum[:, :, :], float(S + i), None, ALU.is_ge))
                    step(V.tensor_tensor(less[:, :, :], subset[:, :, :], over[:, :, :], ALU.subtract))
                    step(V.tensor_tensor(subset[:, :, :], subset[:, :, :], less[:, :, :], ALU.bitwise_and))
                step(V.tensor_scalar(topi[:, :, :], topi[:, :, :], -1.0, float(Q * PAT), ALU.mult, ALU.add))
                if not (isinstance(b, int) and b < 2):
                    dve.wait_ge(s_pool, T * (b - 1))
                V.tensor_tensor(idx[par][:, :, :], topi[:, :, :], subset[:, :, :], ALU.add).then_inc(s_idx, 1)

            def pooled(b, t):
                dve.wait_ge(s_rows[t % 2], 16 * rows_until(b, t))
                V.tensor_reduce(pool[:, t, :], rows[t % 2][:, 0:slots(b), :].rearrange("p r c -> p c r"), AX.X, ALU.max)\
                 .then_inc(s_pool, 1)

            def rest_of_h0(b):
                dve.wait_ge(s_h0hi, b + 1)
                V.scalar_tensor_tensor(h0_lo[:, :, :], h0_r, SCALE, h0_hi[:, :, :], ALU.mult, ALU.subtract)\
                 .then_inc(s_h0lo, 1)

            def hot(b, par, u):
                rank, half = slots(b) + 1 + u // 2, u % 2
                V.tensor_scalar(one_hot[u % 2][:, :, :], adj_t[par][:, :, half * HALF:(half + 1) * HALF], rank + 0.5,
                                None, ALU.is_equal).then_inc(s_hot, 1)

            def first_hot(b, par, u):
                if u == 0:
                    dve.wait_ge(s_rank, RANKED * (b + 1))
                hot(b, par, u)

            def take(b, par, u):
                half = slice(u % 2 * HALF, (u % 2 + 1) * HALF)
                dve.wait_ge(s_pick, units_before(b) + u + 1)
                if u < 2:
                    V.tensor_copy(picked[:, half], ps_a[:, u % 2, :]).then_inc(s_picked, 1)
                else:
                    V.tensor_tensor(picked[:, half], picked[:, half], ps_a[:, u % 2, :], ALU.max).then_inc(s_picked, 1)
                if u + 2 < units(b):
                    hot(b, par, u + 2)

            def takes(b, par, place):
                for u in UNITS_AT[place]:
                    take(b, par, u)

            def layer0_in(d):
                dve.wait_ge(s_pt, d + 1)
                dve.sem_inc(s_gate, 1)
                dve.wait_ge(s_picked, units_before(d + 1))
                V.scalar_tensor_tensor(pool_t, picked[:, :], 1.0 / SCALE, ps_z[:, :, :].rearrange("p a n -> p (a n)"),
                                       ALU.mult, ALU.max).then_inc(s_poolt, 1)

            def layer0(d):
                dve.wait_ge(s_out, 16 * d + 16)
                dve.sem_inc(s_gate, 1)
                dve.wait_ge(s_xs, 16 * d + 16)
                dve.sem_inc(s_gate, 1)
                dve.wait_ge(s_p0, d + 1)
                step(V.scalar_tensor_tensor(x_s[:, :, :], ps_d[:, :].rearrange("p (t c) -> p t c", t=T), 0.0, x_in,
                                            ALU.max, ALU.add))

            def normed(d, layer, tiles=range(T)):
                stats(x_s, tiles)
                rsqrt(y0)
                own = T
                if layer == 3:
                    V.scalar_tensor_tensor(my0[:, :], mv[:, :, 0], -1.0, y0[:, :], ALU.mult, ALU.mult).then_inc(s_my, 1)
                    own = T // 2
                for t in range(own):
                    i = V.tensor_scalar(h[:, t, :], x_s[:, t, :], mv[:, t, 0:1], y0[:, t:t + 1],
                                        ALU.subtract, ALU.mult)
                    if t < own - 1:
                        mark(i)
                    else:
                        i.then_inc(s_h, 1)
                dve.wait_ge(s_chain, done[0])

            def message_parts(d):
                dve.wait_ge(s_hi, d + 1)
                V.tensor_tensor(rest[:, :, :], ps_z[:, :, :].rearrange("p a (t c) -> p (a t) c", t=T // 2), hi[:, :, :],
                                ALU.subtract).then_inc(s_rest, 1)
                dve.wait_ge(s_mid, d + 1)
                V.tensor_tensor(lo[:, :, :], rest[:, :, :], mid[:, :, :], ALU.subtract).then_inc(s_lo, 1)

            def layer1_update(d, par):
                dve.wait_ge(s_up, d + 1)
                step(V.tensor_tensor(upd[:, :, :], ps_d[:, :].rearrange("p (t c) -> p t c", t=T),
                                     b1_s[:, None, :].broadcast_to([P, T, C]), ALU.add))
                dve.wait_ge(s_mask, T * d + T)
                step(V.tensor_scalar(rdeg[:, :], degsum[par][:, :], 1.0 / FP8_BIG, float(N), ALU.mult, ALU.add))
                step(V.tensor_scalar(rdeg[:, :], rdeg[:, :], 1.0, None, ALU.max))
                step(V.reciprocal(rdeg[:, :], rdeg[:, :]))

            def layer1(d):
                dve.wait_ge(s_msg, d + 1)
                for t in range(T):
                    mark(V.scalar_tensor_tensor(upd[:, t, :], ps_z[:, t // 4, (t % 4) * C:(t % 4 + 1) * C],
                                                rdeg[:, t:t + 1], upd[:, t, :], ALU.mult, ALU.add))
                dve.wait_ge(s_chain, done[0])
                step(V.scalar_tensor_tensor(x_s[:, :, :], upd[:, :, :], 0.0, x_s[:, :, :], ALU.max, ALU.add))

            def parts(col, dst, at):
                step(V.tensor_copy(dst[:, :, at], col))
                step(V.tensor_tensor(left[:, :], col, dst[:, :, at], ALU.subtract))
                step(V.tensor_copy(dst[:, :, at + 1], left[:, :]))
                return V.tensor_tensor(dst[:, :, at + 2], left[:, :], dst[:, :, at + 1], ALU.subtract)

            def logits(d, layer):
                dve.wait_ge(s_sd, 4 * d + 2 * (layer - 1))
                dve.sem_inc(s_gate, 1)

            def combine(d, layer, beside):
                for u in range(2 * T):
                    half, m = u // T, u % T
                    dve.wait_ge(s_e, 64 * d + (layer - 2) * 32 + 2 * u + 2)
                    V.tensor_tensor(e_s[half][:, m, :], e_s[half][:, m, :], e_two4[u % 4],
                                    ALU.min if layer == 2 else ALU.max).then_inc(s_em, 1)
                    beside(u)

            def attended(d, layer, half):
                at = slice(half * T // 2, (half + 1) * T // 2)
                dve.wait_ge(s_oc, 16 * d + (layer - 2) * 8 + (half + 1) * T // 2)
                dve.sem_inc(s_gate, 1)
                if layer == 2:
                    step(V.tensor_scalar(left[:, at], att[:, at, C], 0.0, None, ALU.is_equal))
                    step(V.tensor_tensor(rsum[:, at], att[:, at, C], left[:, at], ALU.add))
                else:
                    step(V.tensor_tensor(rsum[:, at], att[:, at, C], empty[:, at], ALU.add))
                step(V.reciprocal(rsum[:, at], rsum[:, at]))
                step(V.tensor_tensor(att[:, at, 0:C], att[:, at, 0:C],
                                     rsum[:, at, None].broadcast_to([P, T // 2, C]), ALU.mult))
                return at

            def layer2_logits(d):
                logits(d, 2)
                mark(V.tensor_scalar(bias1[:, :], sd[:, :, 1], -1.0, None, ALU.mult))
                mark(V.tensor_scalar(bias2[:, :], sd[:, :, 1], -SLOPE, None, ALU.mult))
                parts(sd[:, :, 0], split3, 0).then_inc(s_sp, 1)

            def layer2_end(d, half):
                at = attended(d, 2, half)
                V.tensor_scalar(neg[:, at, :], att[:, at, 0:C], 0.0, None, ALU.min).then_inc(s_neg, 1)
                dve.wait_ge(s_exp, 2 * d + half + 1)
                step(V.scalar_tensor_tensor(neg[:, at, :], att[:, at, 0:C], 0.0, neg[:, at, :], ALU.max, ALU.add))
                step(V.scalar_tensor_tensor(x_s[:, at, :], neg[:, at, :], -1.0, x_s[:, at, :], ALU.add, ALU.add))

            def layer3_logits(d):
                logits(d, 3)
                mark(V.tensor_copy(bias1[:, :], sd[:, :, 1]))
                mark(V.tensor_scalar(bias2[:, :], sd[:, :, 1], SLOPE, None, ALU.mult))
                parts(sd[:, :, 1], split3, 0).then_inc(s_sp, 1)

            def layer3_peaks(d):
                dve.wait_ge(s_rb, d + 1)
                step(V.tensor_reduce(least[:, :], ps_d[:, :], AX.X, ALU.min))
                step(V.tensor_scalar(rel, ps_d[:, :], least[:, 0:1], 1.0, ALU.subtract, ALU.add))
                dve.wait_ge(s_adj, 16 * d + 16)
                for t in range(T):
                    mark(V.tensor_tensor_reduce(out=e_s[t // 4][:, 2 * (t % 4):2 * (t % 4) + 2, :], in0=adj_s[:, t, :],
                                                in1=rel, scale=1.0, scalar=0.0, op0=ALU.mult,
                                                op1=ALU.max, accum_out=wmax[:, t:t + 1]))
                dve.wait_ge(s_chain, done[0])
                mark(V.tensor_scalar(empty[:, :], wmax[:, :], 0.5, None, ALU.is_lt))
                step(V.tensor_scalar(zmax[:, :], wmax[:, :], -1.0, least[:, 0:1], ALU.add, ALU.add))
                step(V.tensor_tensor(zmax[:, :], zmax[:, :], sd[:, :, 0], ALU.add))
                step(V.scalar_tensor_tensor(peak[:, :], zmax[:, :], SLOPE, zmax[:, :], ALU.mult, ALU.max))
                mark(V.tensor_tensor(ucol[:, :], sd[:, :, 0], peak[:, :], ALU.subtract))
                V.scalar_tensor_tensor(vcol[:, :], sd[:, :, 0], SLOPE, peak[:, :], ALU.mult, ALU.subtract).then_inc(s_peak, 1)
                dve.wait_ge(s_peak, d + 1)
                dve.wait_ge(s_chain, done[0])
                step(parts(ucol[:, :], split6, 0))
                parts(vcol[:, :], split6, 3).then_inc(s_sp, 1)

            def layer3_end(d, half):
                at = attended(d, 3, half)
                step(V.tensor_tensor(x_s[:, at, :], att[:, at, 0:C], x_s[:, at, :], ALU.add))
                dve.wait_ge(s_meanc, d + 1)
                for t in range(half * T // 2, (half + 1) * T // 2):
                    i = V.scalar_tensor_tensor(x_s[:, t, :], mean_s[:, :], empty[:, t:t + 1], x_s[:, t, :],
                                               ALU.mult, ALU.add)
                    if t < T - 1:
                        mark(i)
                    else:
                        i.then_inc(s_y, 1)
                dve.wait_ge(s_chain, done[0])

            def body(b, par, d):
                more = not (isinstance(b, int) and b == B - 1)
                nxt = b + 1 if more else None

                def beside2(u):
                    if u == 1:
                        first_hot(b, par, 0)
                    if u == 4:
                        first_hot(b, par, 1)
                    if u in (10, 14) and u // 4 - 2 < len(UNITS_AT["layer2"]):
                        take(b, par, UNITS_AT["layer2"][u // 4 - 2])
                    if more and u in (2, 6, 10):
                        tops(nxt, 2 + u // 4)
                    if u == 7:
                        pooled(b, 2)
                    if u == 12:
                        pooled(b, 3)
                    if more and u == 9:
                        lead_subsets(nxt, 1)

                def beside3(u):
                    if u < len(UNITS_AT["peaks"]):
                        take(b, par, UNITS_AT["peaks"][u])
                    if u >= 6 and u % 4 == 2 and u // 4 - 1 < len(UNITS_AT["layer3"]):
                        take(b, par, UNITS_AT["layer3"][u // 4 - 1])
                    if more and u == 4:
                        tops(nxt, T - 1)
                    if u == 3:
                        pooled(b, 5)
                    if more and u == 7:
                        indices(nxt, 1 - par)
                    if u == 12:
                        pooled(b, 6)

                if d is None:
                    rest_of_h0(b)
                    lead_stats(nxt)
                    pooled(b, 0)
                    first_hot(b, par, 0)
                    first_hot(b, par, 1)
                    for t in range(T):
                        if t < T - 1:
                            for u in range(t * PER_TILE_0, (t + 1) * PER_TILE_0):
                                take(b, par, u)
                        tops(nxt, t)
                        if t == 3:
                            lead_subsets(nxt, 0)
                        if t == 5:
                            lead_subsets(nxt, 1)
                        if t + 1 < T:
                            pooled(b, t + 1)
                    indices(nxt, 1 - par)
                    for u in range((T - 1) * PER_TILE_0, UNITS_0):
                        take(b, par, u)
                else:
                    layer0_in(d)
                    layer0(d)
                    normed(d, 1)
                    if more:
                        tops(nxt, 0)
                        lead_stats(nxt)
                    message_parts(d)
                    if more:
                        tops(nxt, 1)
                    pooled(b, 0)
                    rest_of_h0(b)
                    layer1_update(d, 1 - par)
                    layer1(d)
                    normed(d, 2)
                    if more:
                        lead_subsets(nxt, 0)
                    pooled(b, 1)
                    layer2_logits(d)
                    combine(d, 2, beside2)
                    layer2_end(d, 0)
                    if more:
                        tops(nxt, 5)
                    stats(x_s, range(T // 2))
                    layer2_end(d, 1)
                    normed(d, 3, range(T // 2, T))
                    if more:
                        tops(nxt, 6)
                    takes(b, par, "norm3")
                    layer3_logits(d)
                    pooled(b, 4)
                    layer3_peaks(d)
                    combine(d, 3, beside3)
                    layer3_end(d, 0)
                    pooled(b, T - 1)
                    layer3_end(d, 1)
                clear()

            def lead0():
                lead_stats(0)
                for t in range(T):
                    tops(0, t)
                    if t == 2:
                        lead_subsets(0, 0)
                    if t == 5:
                        lead_subsets(0, 1)
                indices(0, 0)
                clear()

            def finish():
                d = B - 1
                layer0_in(d)
                layer0(d)
                normed(d, 1)
                message_parts(d)
                layer1_update(d, 1)
                layer1(d)
                normed(d, 2)
                layer2_logits(d)
                combine(d, 2, lambda u: None)
                layer2_end(d, 0)
                stats(x_s, range(T // 2))
                layer2_end(d, 1)
                normed(d, 3, range(T // 2, T))
                layer3_logits(d)
                layer3_peaks(d)
                combine(d, 3, lambda u: None)
                layer3_end(d, 0)
                layer3_end(d, 1)

            over_graphs(dve, lead0, body, finish)

        @block.tensor
        def _(pe):
            mm = nc.tensor.matmul
            pe.wait_ge(s_w, 16 * 9)
            pe.wait_ge(s_const, 1)
            nc.tensor.transpose(ps_d[:, 0:P], w2_s[:, 0:C], ident[:, :]).then_inc(s_wt, 1)
            nc.tensor.transpose(ps_d[:, P:2 * P], w3_s, ident[:, :]).then_inc(s_wt, 1)
            pe.wait_ge(s_wc, 2)
            mm(ps_d[:, 0:2], w2t, a2_s[:, :], start=True, stop=True).then_inc(s_wsd, 1)
            mm(ps_d[:, 2:4], w3_s, a3_s[:, :], start=True, stop=True).then_inc(s_wsd, 1)
            pe.wait_ge(s_wsc, 2)

            def transposes(src, dst, tiles=range(T)):
                for t in tiles:
                    last = nc.tensor.transpose(dst(t), src[:, t, :], ident[:, :])
                return last

            def of_projected(t):
                return (pv_d if t < T // 2 else pv_z)[:, t % 4 // 2, t % 2, :]

            def to_z(t):
                return ps_z[:, t // 4, (t % 4) * P:(t % 4 + 1) * P]

            def lead_tile(b, par, k):
                if k < T:
                    lead_transposes(b, k)
                if k > 0:
                    lead_codes(b, par, k - 1)

            def lead_transposes(b, k):
                if k % 2 == 0:
                    i = k // 2
                    pe.wait_ge(s_lead[i % 2], 32 * b + 16 * (i // 2) + 16)
                if not (isinstance(b, int) and T * b + k < 2):
                    pe.wait_ge(s_coded, T * b + k - 1)
                for j in range(T):
                    last = nc.tensor.transpose(ps_t[k % 2][:, j * P:(j + 1) * P],
                                               adj_l[:, k % 4, j * P:(j + 1) * P], ident16[:, :])
                last.then_inc(s_lt, 1)
            def lead_codes(b, par, n):
                codes = ps_t[n % 2][:, :].bitcast(f32)
                pe.wait_ge(s_at, T * b + n + 1)
                for j in range(T):
                    at = adj_t[par][:, j, n * P:(n + 1) * P]
                    mm(codes[:, 32 * j:32 * j + 32], at, weigh[:, :], start=True, stop=True)
                for j in range(T):
                    at = adj_t[par][:, j, n * P:(n + 1) * P]
                    mm(codes[:, Q + 32 * j:Q + 32 * j + 32], at, weigh[:, :], start=True, stop=False)
                    last = mm(codes[:, Q + 32 * j:Q + 32 * j + 32], ones16[:, :], group[:, 32 * j:32 * j + 32],
                              start=False, stop=True)
                last.then_inc(s_code, 1)

            def count(b, par):
                if not (isinstance(b, int) and b == 0):
                    pe.wait_ge(s_picked, units_before(b))
                for j in range(T):
                    for half in range(2):
                        at = slice(half * HALF, (half + 1) * HALF)
                        if j > 0:
                            pe.wait_ge(s_rank, RANKED * b + 2 * (j - 1) + half + 1)
                        last = mm(ps_a[:, half, :], upper[:, :], adj_t[par][:, j, at], start=True, stop=(j == 0))
                        if j > 0:
                            ranked = rank_0[:, at] if j == 1 else adj_t[par][:, j - 2, at]
                            mm(ps_a[:, half, :], last_row[:, :], ranked, start=False, stop=False)
                            last = mm(ps_a[:, half, :], last_half[:, :], adj_t[par][:, j - 1, at], start=False, stop=True)
                        last.then_inc(s_cnt, 1)

            def pick(b, u, quarters=range(4)):
                for q in quarters:
                    if q == 0:
                        pe.wait_ge(s_hot, units_before(b) + u + 1)
                        if not (isinstance(b, int) and b == 0 and u < 2):
                            pe.wait_ge(s_picked, units_before(b) + u - 1)
                    for j in (2 * q, 2 * q + 1):
                        for k, part_k in enumerate((h0_hi, h0_lo)):
                            last = mm(ps_a[:, u % 2, :], part_k[:, j, :], one_hot[u % 2][:, (j - 1) % T, :],
                                      start=(j == 0 and k == 0), stop=(j == T - 1 and k == 1))
                    if q == 3:
                        last.then_inc(s_pick, 1)

            def picks(b, place):
                for u in UNITS_AT[place]:
                    pick(b, u)

            def h0_transposes(b):
                pe.wait_ge(s_h0d, 64 * b + 64)
                transposes(h0_d, to_z).then_inc(s_h0p, 1)

            def h0_in(b, d):
                if d is None:
                    h0_transposes(b)
                pe.wait_ge(s_h0t, b + 1)
                if d is not None:
                    pe.wait_ge(s_oc, 16 * d + 16)
                for t in range(T):
                    mm(to_d(t), h_t[:, t * P:(t + 1) * P], w0_s[:, 0, :], start=(t % 4 == 0), stop=False)
                for t in range(T):
                    mm(to_d(t), inv_p[:, :], b0_s[:, :], start=False, stop=False)

            def layer0(d, par):
                pe.wait_ge(s_pool, T * d + T)
                transposes(pool, to_z).then_inc(s_pt, 1)
                pe.wait_ge(s_poolt, d + 1)
                for t in range(T):
                    last = mm(to_d(t), pool_t[:, t * P:(t + 1) * P], w0_s[:, 1, :], start=False, stop=(t % 4 == 3))
                last.then_inc(s_p0, 1)

            def h_transposes(d, layer):
                pe.wait_ge(s_h, 3 * d + layer)
                transposes(h, to_d, range(T // 2))
                if layer == 3:
                    pe.wait_ge(s_h2, d + 1)
                transposes(h, to_d, range(T // 2, T)).then_inc(s_ht, 1)
                pe.wait_ge(s_htc, 3 * d + layer)

            def project(dst, w):
                for t in range(T):
                    last = mm(dst(t), h_t[:, t * P:(t + 1) * P], w, start=True, stop=True)
                return last

            def layer1_in(d):
                h_transposes(d, 1)
                project(to_z, w1m_s[:, :]).then_inc(s_hm, 1)
                project(to_d, w1u_s[:, :]).then_inc(s_up, 1)

            def layer1(d):
                pe.wait_ge(s_adj, 16 * d + 16)
                pe.wait_ge(s_rest, d + 1)
                for k, part_k in enumerate((hi, mid, lo)):
                    if k == 1:
                        pe.wait_ge(s_mid, d + 1)
                    if k == 2:
                        pe.wait_ge(s_lo, d + 1)
                    for j in range(T):
                        for i in range(T):
                            last = mm(to_z(j), adj_s[:, i, j * P:(j + 1) * P], part_k[:, i, :],
                                      start=(j % 4 == 0 and i == 0 and k == 0), stop=(j % 4 == 3 and i == T - 1 and k == 2))
                last.then_inc(s_msg, 1)

            def attention_in(d, layer, w):
                h_transposes(d, layer)
                for t in range(T):
                    last = mm(of_projected(t), h_t[:, t * P:(t + 1) * P], w, start=True, stop=True)
                last.then_inc(s_pv, 1)

            def part_rows(value, split, n):
                pe.wait_ge(s_sp, value)
                for t in range(T):
                    last = nc.tensor.transpose(ps_zb[0:n, t * P:(t + 1) * P], split[:, t, 0:n], identb[:, :])
                last.then_inc(s_spt, 1)
                pe.wait_ge(s_row, value)

            def unit(par, slot, gain, sel, row, half, m):
                at = slice(half * HALF, (half + 1) * HALF)
                mm(ps_z[:, slot, :], sel[:, :], row[:, at], start=True, stop=False)
                mm(ps_z[:, slot, :], gain[:, :], mask[par][:, m, at], start=False, stop=True).then_inc(s_z, 1)

            def sums(d, layer, half, n):
                q = half * (T // 2) + n
                if n == 0:
                    pe.wait_ge(s_em, 32 * d + (layer - 2) * 16 + (half + 1) * T)
                o = 16 * d + (layer - 2) * 8 + q
                if q >= 2:
                    pe.wait_ge(s_oc, o - 1)
                for m in range(T):
                    last = mm(ps_d[:, (q % 2) * HALF:(q % 2) * HALF + C + 1], e_s[half][:, m, n * P:(n + 1) * P],
                              vmat[:, m, :], start=(m == 0), stop=(m == T - 1))
                last.then_inc(s_o, 1)

            def layer2(d, par, b, g):
                attention_in(d, 2, w2_s[:, :])
                pe.wait_ge(s_vm, 4 * d + 1)
                part_rows(3 * d + 1, split3, 3)
                pe.wait_ge(s_vm, 4 * d + 2)
                for u in range(2 * T):
                    if u >= 2:
                        pe.wait_ge(s_e, 64 * d + 2 * (u - 1))
                    unit(par, u % 2, mask_neg, sel_a, row, u // T, u % T)
                    if b is not None and u % 4 == 1:
                        lead_codes(b, par, 2 + u // 4)
                    if b is not None and u % 4 == 3:
                        lead_transposes(b, 3 + u // 4)
                    if g is not None and u >= 5 and (u - 5) // 4 < len(UNITS_AT["layer2"]):
                        pick(g, UNITS_AT["layer2"][(u - 5) // 4], ((u - 5) % 4,))
                    if u >= T + 1 and u % 2 == 1:
                        sums(d, 2, 0, (u - T) // 2)
                for n in range(T // 2):
                    sums(d, 2, 1, n)

            def layer3(d, par, b, g):
                attention_in(d, 3, w3t[:, :])
                pe.wait_ge(s_vm, 4 * d + 3)
                part_rows(3 * d + 2, split3, 3)
                pe.wait_ge(s_vm, 4 * d + 4)
                for half in range(2):
                    last = mm(ps_d[:, half * HALF:(half + 1) * HALF], sel_a[:, :],
                              row[:, half * HALF:(half + 1) * HALF], start=True, stop=True)
                last.then_inc(s_rb, 1)
                for m in range(T):
                    last = mm(ps_z[:, 0, 0:C], inv_p[:, :], vmat[:, m, 0:C], start=(m == 0), stop=(m == T - 1))
                last.then_inc(s_mean, 1)
                if b is not None:
                    lead_tile(b, par, T)
                if g is not None:
                    picks(g, "peaks")
                pe.wait_ge(s_meanc, d + 1)
                part_rows(3 * d + 3, split6, 6)
                for u in range(2 * T):
                    e = 64 * d + 32 + 2 * u
                    if u >= 1:
                        pe.wait_ge(s_e, e - 1)
                    unit(par, 0, mask_pos, sel_a, row, u // T, u % T)
                    if u >= 1:
                        pe.wait_ge(s_e, e)
                    unit(par, 1, mask_pos, sel_b, row, u // T, u % T)
                    if g is not None and u >= 2 and (u - 2) // 4 < len(UNITS_AT["layer3"]):
                        pick(g, UNITS_AT["layer3"][(u - 2) // 4], ((u - 2) % 4,))
                    if u >= T + 1 and u % 2 == 1:
                        sums(d, 3, 0, (u - T) // 2)
                for n in range(T // 2):
                    sums(d, 3, 1, n)
                    if n == 1 and g is not None:
                        h0_transposes(g)

            def dense(d, par, b, g):
                layer0(d, par)
                if b is not None:
                    lead_tile(b, par, 0)
                    lead_tile(b, par, 1)
                layer1_in(d)
                if b is not None:
                    lead_tile(b, par, 2)
                layer1(d)
                if g is not None:
                    count(g, 1 - par)
                layer2(d, par, b, g)
                if b is not None:
                    lead_tile(b, par, 7)
                if g is not None:
                    picks(g, "norm3")
                layer3(d, par, b, g)

            def body(b, par, d):
                more = not (isinstance(b, int) and b == B - 1)
                if d is not None:
                    dense(d, 1 - par, b + 1 if more else None, b)
                else:
                    count(b, par)
                    for k in range(T):
                        lead_tile(b + 1, 1 - par, k)
                        if k == T - 1:
                            lead_tile(b + 1, 1 - par, T)
                        for u in range(k * PER_TILE_0, (k + 1) * PER_TILE_0 if k < T - 1 else UNITS_0):
                            pick(b, u)
                h0_in(b, d)

            def lead0():
                for k in range(T + 1):
                    lead_tile(0, 0, k)

            over_graphs(pe, lead0, body, lambda: dense(B - 1, 1, None, None))


_INS = ["x", "adj", "L0_gnn_W", "L0_gnn_b", "L1_gnn_W_msg", "L1_gnn_W_upd", "L1_gnn_bias", "L2_gnn_W",
        "L2_gnn_a", "L3_gnn_W", "L3_gnn_a"]


def kernel(**inputs):
    import concourse.bacc as bacc
    from concourse.bass_utils import run_bass_kernel_spmd

    nc = bacc.Bacc("TRN2", target_bir_lowering=False, num_devices=1)
    arrays, args = {}, []
    for name in _INS:
        a = np.ascontiguousarray(inputs[name])
        arrays[f"in_{name}"] = a
        args.append(nc.dram_tensor(f"in_{name}", a.shape, DT.from_np(a.dtype), kind="ExternalInput").ap())
    args.append(nc.dram_tensor("out_x", (B, N, C), DT.float32, kind="ExternalOutput").ap())
    build(nc, *args)
    r = run_bass_kernel_spmd(nc, [arrays], core_ids=[0])
    return r.results[0]["out_x"]
```
